# Optimizing a Trainium2 kernel written in Bass

```python
import numpy as np
import jax
import jax.numpy as jnp

def _softmax(x, axis=-1):
    return jax.nn.softmax(x, axis=axis)

def _gelu(x):
    return jax.nn.gelu(x, approximate=True)

def _silu(x):
    return jax.nn.silu(x)

def _sigmoid(x):
    return jax.nn.sigmoid(x)

def _layernorm(x, axis=-1, eps=1e-05):
    m = jnp.mean(x, axis=axis, keepdims=True)
    v = jnp.var(x, axis=axis, keepdims=True)
    return (x - m) / jnp.sqrt(v + eps)

def _scatter_add(tgt, idx, src, axis=0):
    return tgt.at[idx].add(src)

def _segment_sum(src, seg, n):
    return jax.ops.segment_sum(src, seg, n)
kernel_name = 'mk_gnn_resnorm_d2_gnn_r16_25a2c8'

def setup_inputs(seed: int=0):
    np.random.seed(seed)
    _w = jnp.asarray

    def _rec_inputs():
        import jax
        import jax.numpy as jnp
        _gk = jax.random.key(seed)
        x = -0.0003713 + 1 * jax.random.normal(jax.random.fold_in(_gk, 1), (3125, 256), jnp.float32)
        _s = jax.random.randint(jax.random.fold_in(_gk, 2), (50000,), 0, 3125, jnp.int32)
        _d = jax.random.randint(jax.random.fold_in(_gk, 3), (50000,), 0, 3125, jnp.int32)
        _loop = jnp.arange(3125, dtype=jnp.int32)
        src = jnp.concatenate([_s, _d, _loop])
        dst = jnp.concatenate([_d, _s, _loop])
        _o = jnp.argsort(dst, stable=True)
        src = src[_o]
        dst = dst[_o]
        return (x, src, dst)
    x, src, dst = _rec_inputs()

    def _L0_gnn_setup():
        import jax, jax.numpy as jnp
        import numpy as np
        import math
        N_NODES = 3125
        N_EDGES = 100000
        C = 256
        H = 8
        HD = C // H

        def _layernorm(x, g, b, eps=1e-05):
            mu = jnp.mean(x, axis=-1, keepdims=True)
            var = jnp.mean(jnp.square(x - mu), axis=-1, keepdims=True)
            return (x - mu) * jax.lax.rsqrt(var + eps) * g + b
        key = jax.random.key(seed)
        ks = jax.random.split(key, 16)
        s = 0.02
        d = {'feat': jax.random.normal(ks[0], (N_NODES, C), jnp.float32), 'edge_src': jax.random.randint(ks[1], (N_EDGES,), 0, N_NODES), 'edge_dst': jax.random.randint(ks[2], (N_EDGES,), 0, N_NODES), 'Wq': jax.random.normal(ks[3], (C, C), jnp.float32) * s, 'bq': jnp.zeros((C,), jnp.float32), 'Wk': jax.random.normal(ks[4], (C, C), jnp.float32) * s, 'bk': jnp.zeros((C,), jnp.float32), 'Wv': jax.random.normal(ks[5], (C, C), jnp.float32) * s, 'bv': jnp.zeros((C,), jnp.float32), 'Wp': jax.random.normal(ks[6], (C, C), jnp.float32) * s, 'bp': jnp.zeros((C,), jnp.float32), 'ln_g': jnp.ones((C,), jnp.float32), 'ln_b': jnp.zeros((C,), jnp.float32), 'W1': jax.random.normal(ks[7], (4 * C, C), jnp.float32) * s, 'b1': jnp.zeros((4 * C,), jnp.float32), 'W2': jax.random.normal(ks[8], (C, 4 * C), jnp.float32) * s, 'b2': jnp.zeros((C,), jnp.float32)}
        return d
    _L0_gnn_all = _L0_gnn_setup()
    _L0_gnn_in = {k: v for k, v in _L0_gnn_all.items() if k in ('Wq', 'bq', 'Wk', 'bk', 'Wv', 'bv', 'Wp', 'bp', 'ln_g', 'ln_b', 'W1', 'b1', 'W2', 'b2')}
    del _L0_gnn_all

    def _L1_gnn_setup():
        import jax, jax.numpy as jnp
        import numpy as np
        N_NODES = 625
        N_EDGES = 20000
        D_IN = 256
        D_OUT = 256
        NEG_SLOPE = 0.2
        key = jax.random.key(seed)
        ks = jax.random.split(key, 8)
        feature = jax.random.normal(ks[0], (N_NODES, D_IN), dtype=jnp.float32)
        src = jax.random.randint(ks[1], (N_EDGES,), 0, N_NODES, dtype=jnp.int32)
        dst = jax.random.randint(ks[2], (N_EDGES,), 0, N_NODES, dtype=jnp.int32)
        s = 1.0 / np.sqrt(D_IN)
        W_s = jax.random.normal(ks[3], (D_OUT, D_IN), dtype=jnp.float32) * s
        W_t = jax.random.normal(ks[4], (D_OUT, D_IN), dtype=jnp.float32) * s
        W_attn = jax.random.normal(ks[5], (1, D_OUT), dtype=jnp.float32) * (1.0 / np.sqrt(D_OUT))
        W_fc = jax.random.normal(ks[6], (D_OUT, D_IN), dtype=jnp.float32) * s
        b_fc = jnp.zeros((D_OUT,), dtype=jnp.float32)
        return {'feature': feature, 'src': src, 'dst': dst, 'W_s': W_s, 'W_t': W_t, 'W_attn': W_attn, 'W_fc': W_fc, 'b_fc': b_fc}
    _L1_gnn_all = _L1_gnn_setup()
    _L1_gnn_in = {k: v for k, v in _L1_gnn_all.items() if k in ('W_s', 'W_t', 'W_attn', 'W_fc', 'b_fc')}
    del _L1_gnn_all
    return {'x': x, 'src': src, 'dst': dst, 'L0_gnn_Wq': _L0_gnn_in['Wq'], 'L0_gnn_bq': _L0_gnn_in['bq'], 'L0_gnn_Wk': _L0_gnn_in['Wk'], 'L0_gnn_bk': _L0_gnn_in['bk'], 'L0_gnn_Wv': _L0_gnn_in['Wv'], 'L0_gnn_bv': _L0_gnn_in['bv'], 'L0_gnn_Wp': _L0_gnn_in['Wp'], 'L0_gnn_bp': _L0_gnn_in['bp'], 'L0_gnn_ln_g': _L0_gnn_in['ln_g'], 'L0_gnn_ln_b': _L0_gnn_in['ln_b'], 'L0_gnn_W1': _L0_gnn_in['W1'], 'L0_gnn_b1': _L0_gnn_in['b1'], 'L0_gnn_W2': _L0_gnn_in['W2'], 'L0_gnn_b2': _L0_gnn_in['b2'], 'L1_gnn_W_s': _L1_gnn_in['W_s'], 'L1_gnn_W_t': _L1_gnn_in['W_t'], 'L1_gnn_W_attn': _L1_gnn_in['W_attn'], 'L1_gnn_W_fc': _L1_gnn_in['W_fc'], 'L1_gnn_b_fc': _L1_gnn_in['b_fc']}

def reference(x, src, dst, L0_gnn_Wq, L0_gnn_bq, L0_gnn_Wk, L0_gnn_bk, L0_gnn_Wv, L0_gnn_bv, L0_gnn_Wp, L0_gnn_bp, L0_gnn_ln_g, L0_gnn_ln_b, L0_gnn_W1, L0_gnn_b1, L0_gnn_W2, L0_gnn_b2, L1_gnn_W_s, L1_gnn_W_t, L1_gnn_W_attn, L1_gnn_W_fc, L1_gnn_b_fc):
    import jax
    import jax.numpy as jnp

    def _L0_gnn_ref(feat, edge_src, edge_dst, Wq, bq, Wk, bk, Wv, bv, Wp, bp, ln_g, ln_b, W1, b1, W2, b2):
        import jax, jax.numpy as jnp
        import numpy as np
        import math
        N_NODES = 3125
        N_EDGES = 100000
        C = 256
        H = 8
        HD = C // H

        def _layernorm(x, g, b, eps=1e-05):
            mu = jnp.mean(x, axis=-1, keepdims=True)
            var = jnp.mean(jnp.square(x - mu), axis=-1, keepdims=True)
            return (x - mu) * jax.lax.rsqrt(var + eps) * g + b
        n = feat.shape[0]
        q = (feat @ Wq.T + bq).reshape(n, H, HD)
        k = (feat @ Wk.T + bk).reshape(n, H, HD)
        v = (feat @ Wv.T + bv).reshape(n, H, HD)
        score = jnp.einsum('ehd,ehd->eh', q[edge_dst], k[edge_src])
        score = jnp.clip(score / math.sqrt(HD), -10.0, 10.0)
        smax = jax.ops.segment_max(score, edge_dst, num_segments=n)
        smax = jnp.where(jnp.isfinite(smax), smax, 0.0)
        ex = jnp.exp(score - smax[edge_dst])
        den = jax.ops.segment_sum(ex, edge_dst, num_segments=n)
        alpha = ex / den[edge_dst]
        wv = jax.ops.segment_sum(alpha[:, :, None] * v[edge_src], edge_dst, num_segments=n).reshape(n, C)
        y = wv @ Wp.T + bp
        x = feat + y
        h = _layernorm(x, ln_g, ln_b)
        h = jax.nn.gelu(h @ W1.T + b1, approximate=False) @ W2.T + b2
        return x + h

    def _L1_gnn_ref(feature, src, dst, W_s, W_t, W_attn, W_fc, b_fc):
        import jax, jax.numpy as jnp
        import numpy as np
        N_NODES = 625
        N_EDGES = 20000
        D_IN = 256
        D_OUT = 256
        NEG_SLOPE = 0.2
        n = feature.shape[0]
        proj_s = feature @ W_s.T
        proj_t = feature @ W_t.T
        z = proj_s[src] + proj_t[dst]
        z = jnp.where(z >= 0, z, NEG_SLOPE * z)
        e = (z @ W_attn.T)[:, 0]
        m = jax.ops.segment_max(e, src, num_segments=n)
        m = jnp.where(jnp.isfinite(m), m, 0.0)
        e_exp = jnp.exp(e - m[src])
        denom = jax.ops.segment_sum(e_exp, src, num_segments=n)
        alpha = e_exp / denom[src]
        msg = feature[src] * alpha[:, None]
        agg = jax.ops.segment_sum(msg, dst, num_segments=n)
        return agg @ W_fc.T + b_fc
    x = _layernorm(x + _L0_gnn_ref(x, src, dst, L0_gnn_Wq, L0_gnn_bq, L0_gnn_Wk, L0_gnn_bk, L0_gnn_Wv, L0_gnn_bv, L0_gnn_Wp, L0_gnn_bp, L0_gnn_ln_g, L0_gnn_ln_b, L0_gnn_W1, L0_gnn_b1, L0_gnn_W2, L0_gnn_b2), axis=-1)
    x = _layernorm(x + _L1_gnn_ref(x, src, dst, L1_gnn_W_s, L1_gnn_W_t, L1_gnn_W_attn, L1_gnn_W_fc, L1_gnn_b_fc), axis=-1)
    return x

_drawn_inputs = setup_inputs


def setup_inputs(seed=0):
    import zlib

    import numpy as np

    out = dict(_drawn_inputs(seed))
    spreads = {'L0_gnn_bq': (0.0, 0.8),
     'L0_gnn_bk': (0.0, 0.8),
     'L0_gnn_bv': (0.0, 0.319),
     'L0_gnn_bp': (0.0, 0.1),
     'L0_gnn_ln_g': (1.0, 0.6),
     'L0_gnn_ln_b': (0.0, 0.8),
     'L0_gnn_b1': (0.0, 0.348),
     'L0_gnn_b2': (0.0, 0.1),
     'L1_gnn_b_fc': (0.0, 0.1)}
    factors = {'L0_gnn_Wq': 8.0, 'L0_gnn_Wk': 8.0, 'L0_gnn_Wv': 5.967}
    for name, (base, spread) in spreads.items():
        noise = np.random.default_rng([zlib.crc32(name.encode()), seed]).standard_normal(out[name].shape)
        drawn = base * np.exp(spread * noise) if base else spread * noise
        out[name] = jnp.asarray(drawn.astype(out[name].dtype))
    for name, factor in factors.items():
        out[name] = (out[name] * factor).astype(out[name].dtype)
    return out
```

```python
from contextlib import ExitStack

import numpy as np

import concourse.bass as bass
from concourse import mybir

ALU = mybir.AluOpType
ACT = mybir.ActivationFunctionType
AX = mybir.AxisListType.X
F32 = mybir.dt.float32
BF16 = mybir.dt.bfloat16
I32 = mybir.dt.int32

P = 128
N_NODES = 3125
C = 256
H = 8
HD = C // H
FF = 4 * C
KC = C // P
NF = FF // P
E_DRAWN = 50000
N_EDGES = 2 * E_DRAWN + N_NODES
W = -(-N_NODES // P)
NP = W * P
FAKE = NP - 1
T = -(-N_EDGES // P)
TB = -(-T // P)
TPAD = TB * P
G = 6
PAIRS = G // 2
CW = C + 2
DT = 13
NB = 5
EPS = 1e-5
SLOPE = 0.2
CLIP = 10.0 * float(HD) ** 0.5
SCORE_SCALE = 1.0 / float(HD) ** 0.5
FAR = 3.0e38
SPREAD = 60.0
assert T % DT == 0 and W % NB == 0 and TPAD >= T + G


def build(nc, io):
    ctx = ExitStack()
    with ctx:
        def sb(name, shape, dt=F32):
            return ctx.enter_context(nc.sbuf_tensor("sb_" + name, shape, dt))

        def psum(name, shape, dt=F32):
            return ctx.enter_context(nc.psum_tensor("ps_" + name, shape, dt))

        def sem(name):
            return ctx.enter_context(nc.semaphore(name))

        def dram(name, shape, dt=F32):
            return nc.dram_tensor(name, shape, dt, kind="Internal").ap()

        kv_rows = dram("kv_rows", [NP, 2 * C])
        proj_rows = dram("proj_rows", [NP, CW])
        feat_rows = dram("feat_rows", [NP, C])

        iota = sb("iota", [P, P])
        ident = sb("ident", [P, P])
        wlo = sb("wlo", [P, W])
        tcon = sb("tcon", [P, 4, W, TB])
        zeros = sb("zeros", [1, P + 2 * C])
        wqkv = sb("wqkv", [P, KC, 3 * C])
        wp = sb("wp", [P, KC, C])
        w1 = sb("w1", [P, KC, FF])
        w2 = sb("w2", [P, NF, C])
        wst = sb("wst", [P, KC, 2 * C])
        wfc = sb("wfc", [P, KC, C])
        bqkv = sb("bqkv", [P, 3 * C])
        bp = sb("bp", [P, C])
        b1 = sb("b1", [P, NF])
        b2 = sb("b2", [P, C])
        bfc = sb("bfc", [P, C])
        lng = sb("lng", [P, KC])
        lnb = sb("lnb", [P, KC])
        attn = sb("attn", [P, C])
        attn_lo = sb("attn_lo", [P, C])
        attn_hi = sb("attn_hi", [P, C])
        eps = sb("eps", [P, 1])

        src_i = sb("src_i", [P, TPAD], I32)
        dst_i = sb("dst_i", [P, TPAD], I32)
        dst_f = sb("dst_f", [P, TPAD])
        src_f = sb("src_f", [P, TPAD])
        src_hi = sb("src_hi", [P, TPAD])
        src_lo = sb("src_lo", [P, TPAD])
        e_all = sb("e_all", [P, TPAD])

        x_w = sb("x_w", [P, C])
        x1 = sb("x1", [P, W, C])
        wide = sb("wide", [P, W, CW])
        parts = sb("parts", [P, W, 3, CW], BF16)

        tile_lo = sb("tile_lo", [P, TB])
        tile_hi = sb("tile_hi", [P, TB])
        hit = sb("hit", [P, W, TB])
        hit2 = sb("hit2", [P, 2, W, TB])
        span = sb("span", [P, 2, W])
        span_all = sb("span_all", [P, 2, W])
        wf = sb("wf", [1, 6, W])
        wtab = sb("wtab", [1, 4 * W], I32)

        gat = sb("gat", [P, G, 2 * C])
        idx = sb("idx", [P, G], I32)
        dst_g = sb("dst_g", [P, G])
        ex_g = sb("ex_g", [P, G])
        onehot = sb("onehot", [P, G, P])
        onehot_t = sb("onehot_t", [P, G, P], BF16)
        prod = sb("prod", [P, 2, 2 * CW])
        score = sb("score", [P, 2, 2, H])
        msg = sb("msg", [P, G, C + H])
        zbuf = msg[:, :, 0:CW]
        dots = sb("dots", [P, 3, G])
        xt = sb("xt", [P, NB, KC, P])

        den = sb("den", [P, 3, H])
        agg = sb("agg", [P, C])
        tr = sb("tr", [P, KC, P])
        xm = sb("xm", [P, C])
        xs = sb("xs", [P, C])
        hn = sb("hn", [P, C])
        hid = sb("hid", [P, NF, P])
        row = sb("row", [P, CW])
        stats = sb("stats", [P, 6])
        mv = sb("mv", [P, 2])
        rstd = sb("rstd", [P, 2])
        denom = sb("denom", [P, 3, W])
        rng = sb("rng", [P, 2])
        rng_all = sb("rng_all", [P, 2])
        shift = sb("shift", [P, 1])
        slow_i = sb("slow_i", [1, 1], I32)

        px = psum("px", [P, 4, 512])
        pt = psum("pt", [P, 2, 512])
        pa = psum("pa", [P, 512])
        pnb = psum("pn", [P, 512])
        pn = pnb[:].rearrange("p (a c) -> p a c", a=2)

        s_const = sem("s_const")
        s_graph = sem("s_graph")
        block = ctx.enter_context(nc.Block())

        tables = sem("tables")
        span_red = sem("span_red")
        wtab_done = sem("wtab_done")
        xt_in = [sem(f"xt_in{s}") for s in range(NB)]
        xt_used = sem("xt_used")
        qkv_out = sem("qkv_out")
        kv_row_ready = sem("kv_row_ready")
        kv_stored = [sem(f"kv_stored{s}") for s in range(NB)]
        split_v = sem("split_v")
        q_ready = sem("q_ready")
        gathered = [[sem(f"gathered{L}_{j}") for j in range(G)] for L in range(3)]
        idx_set = [sem(f"idx_set{L}") for L in range(3)]
        idx_seen = sem("idx_seen")
        dve_seen = sem("dve_seen")
        slots_free = [sem(f"slots_free{L}") for L in range(3)]
        hot = [sem(f"hot{L}") for L in range(3)]
        hot_t = [sem(f"hot_t{L}") for L in range(2)]
        hot_c = [sem(f"hot_c{L}") for L in range(2)]
        expd = [sem(f"expd{L}") for L in range(2)]
        gdst = [sem(f"gdst{L}") for L in range(3)]
        mul1 = sem("mul1")
        red1 = sem("red1")
        clp1 = sem("clp1")
        exp1 = sem("exp1")
        msg1 = sem("msg1")
        summed = [sem(f"summed{L}") for L in (0, 1)]
        opened = [sem(f"opened{L}") for L in (0, 1)]
        nv = sem("nv")
        na = sem("na")
        nt = sem("nt")
        proj_stored = sem("proj_stored")
        x_in = sem("x_in")
        t_ready = sem("t_ready")
        zs = sem("zs")
        ev = sem("ev")
        ea = sem("ea")
        ep = sem("ep")
        slow_flag = sem("slow_flag")
        sv = sem("sv")
        slow_max = sem("slow_max")
        slow_all = sem("slow_all")
        dv = sem("dv")
        dpe = sem("dpe")
        fv = sem("fv")
        feat_stored = sem("feat_stored")
        gv = sem("gv")
        ga = sem("ga")
        gt = sem("gt")
        out_stored = sem("out_stored")

        CONSTS = [
            (iota[:], io["c_iota"]), (ident[:], io["c_ident"]), (wlo[:], io["c_wlo"]),
            (tcon[:], io["c_tcon"]), (wqkv[:], io["wqkv"].rearrange("(k p) n -> p k n", p=P)),
            (wp[:], io["wp"].rearrange("(k p) n -> p k n", p=P)),
            (w1[:], io["w1"].rearrange("(k p) n -> p k n", p=P)),
            (w2[:], io["w2"].rearrange("(k p) n -> p k n", p=P)),
            (wst[:], io["wst"].rearrange("(k p) n -> p k n", p=P)),
            (wfc[:], io["wfc"].rearrange("(k p) n -> p k n", p=P)),
            (bqkv[:], io["bqkv"].partition_broadcast(P)), (bp[:], io["bp"].partition_broadcast(P)),
            (b1[:], io["b1"]), (b2[:], io["b2"].partition_broadcast(P)),
            (bfc[:], io["bfc"].partition_broadcast(P)), (lng[:], io["lng"]), (lnb[:], io["lnb"]),
            (attn[:], io["attn"].partition_broadcast(P)),
        ]
        GRAPH = [
            (src_i[:], io["src"]), (dst_i[:], io["dst"]),
            (x1[:].rearrange("p w c -> p (w c)")[:, 0:TPAD].bitcast(I32).rearrange("p (b e) -> p b e", b=TB),
             io["dst_r"].rearrange("(b p) e -> p b e", p=P)),
        ]
        dst_rows = x1[:].rearrange("p w c -> p (w c)")[:, 0:TPAD].bitcast(I32).rearrange("p (b e) -> p b e", b=TB)
        CONST_ALL = 16 * len(CONSTS)
        GRAPH_ALL = 16 * len(GRAPH)

        def window(eng, w):
            first = eng.value_load(wtab[0:1, bass.ds(w * 4, 1)], min_val=0, max_val=T - 1)
            groups = eng.value_load(wtab[0:1, bass.ds(w * 4 + 1, 1)], min_val=1, max_val=-(-T // G) + 1)
            before = eng.value_load(wtab[0:1, bass.ds(w * 4 + 2, 1)], min_val=0, max_val=W * (-(-T // G) + 1))
            return first, groups, before

        def first_tile(first, k):
            return nc.s_assert_within(first + k * G, 0, T - 1, skip_runtime_bounds_check_because="a window's groups start at its tiles, which are below T")

        def steps(names):
            return {n: i + 1 for i, n in enumerate(names)}

        NVS = steps(["den0", "den1", "den2", "agg", "xm0", "xm1", "st0", "mv0", "rs0", "h",
                     "xs0", "xs1", "xs2", "st1", "mv1", "rs1", "x1", "dot_s", "dot_t", "proj_row"])
        NV = len(NVS)
        NAS = steps(["aggT", "sqrt0", "hT", "hid", "sqrt1", "x1T", "x1_all", "t_row", "proj_row"])
        NA = len(NAS)
        NTS = steps(["aggT", "y", "hT", "hid", "mlp", "x1T", "proj"])
        NT = len(NTS)
        GVS = steps(["agg", "y0", "y1", "st", "mv", "rs", "out"])
        GV = len(GVS)
        GAS = steps(["aggT", "sqrt"])
        GA = len(GAS)
        GTS = steps(["aggT", "y"])
        GT = len(GTS)
        FVS = steps(["den0", "den1", "den2", "feat"])
        gat_row = row[:]
        feats = wide[:, :, 0:C]

        spare = parts[:].rearrange("p w a c -> p (w a c)").bitcast(F32)
        node_max = spare[:, 0:NP]
        node_max_all = spare[:, NP:2 * NP]
        lo_hot = spare[:, 0:2 * DT * P].rearrange("p (b j n) -> p b j n", b=2, j=DT)
        hi_hot = spare[:, 2 * DT * P:2 * DT * (P + W)].rearrange("p (b j n) -> p b j n", b=2, j=DT)

        @block.sync
        def _(sp):
            for dst_ap, src_ap in GRAPH:
                sp.dma_start(dst_ap, src_ap).then_inc(s_graph, 16)
            for dst_ap, src_ap in CONSTS:
                sp.dma_start(dst_ap, src_ap).then_inc(s_const, 16)
            sp.sem_inc(xt_used, 1)
            with sp.Fori(0, W // NB) as it:
                for s in range(NB):
                    if s == 0:
                        sp.wait_ge(xt_used, it * NB + 1)
                    sp.dma_start(xt[:, s], io["xt"][bass.ds(it * NB + s, 1)].rearrange("o p k n -> p (o k) n")).then_inc(xt_in[s], 16)
            with sp.Fori(0, W) as w:
                sp.wait_ge(opened[0], w + 1)
                sp.dma_start(x_w[:], io["x"][bass.ds(w * P, P), :]).then_inc(x_in, 16)
                sp.wait_ge(nv, w * NV + NVS["proj_row"])
                sp.wait_ge(na, w * NA + NAS["proj_row"])
                sp.dma_start(proj_rows[bass.ds(w * P, P), :], gat_row).then_inc(proj_stored, 16)
            sp.wait_ge(fv, FVS["feat"])
            sp.dma_start(feat_rows.rearrange("(w p) c -> p w c", p=P), feats).then_inc(feat_stored, 16)
            with sp.Fori(0, W - 1) as w:
                sp.wait_ge(gv, w * GV + GV)
                sp.dma_start(io["out"][bass.ds(w * P, P), :], hn[:]).then_inc(out_stored, 16)
            sp.wait_ge(gv, W * GV)
            sp.dma_start(io["out"][(W - 1) * P:N_NODES, :], hn[0:N_NODES - (W - 1) * P, :]).then_inc(out_stored, 16)
            sp.wait_ge(out_stored, 16 * W + 1)

        @block.gpsimd
        def _(pool):
            pool.wait_ge(tables, 9)
            pool.partition_all_reduce(span_all[:].rearrange("p a w -> p (a w)"),
                                      span[:].rearrange("p a w -> p (a w)"), P,
                                      bass.bass_isa.ReduceOp.max).then_inc(span_red, 1)
            pool.wait_ge(wtab_done, 1)

            def gathers(L, rows, width):
                with pool.Fori(0, W) as w:
                    first, groups, before = window(pool, w)
                    with pool.Fori(0, groups) as k:
                        v = pool.snap(before + k)
                        t0 = first_tile(first, k)
                        for p in range(PAIRS):
                            pool.wait_ge(slots_free[L], v * PAIRS + p + 1)
                            pool.tensor_copy(idx[:, 2 * p:2 * p + 2], src_i[:, bass.ds(t0 + 2 * p, 2)]).then_inc(idx_set[L], 1)
                            pool.wait_ge(idx_set[L], v * PAIRS + p + 1)
                            pool.sem_inc(idx_seen, 1)
                            for j in (2 * p, 2 * p + 1):
                                pool.indirect_dma_start(
                                    out=gat[:, j, 0:width], out_offset=None, in_=rows,
                                    in_offset=bass.IndirectOffsetOnAxis(ap=idx[:, j:j + 1], axis=0)).then_inc(gathered[L][j], 16)

            for s in range(NB):
                pool.wait_ge(kv_stored[s], 16 * (W // NB) + 1)
            gathers(0, kv_rows, 2 * C)
            pool.wait_ge(proj_stored, 16 * W + 1)
            gathers(1, proj_rows, CW)
            pool.wait_ge(ev, 2)
            pool.partition_all_reduce(rng_all[:], rng[:], P, bass.bass_isa.ReduceOp.max).then_inc(ep, 1)
            pool.wait_ge(slow_flag, 1)
            slow = pool.alloc_register("slow_pool")
            pool.reg_load(slow, slow_i[0:1, 0:1])
            with pool.If_ne(slow, 0):
                pool.wait_ge(slow_max, 1)
                pool.partition_all_reduce(node_max_all, node_max, P, bass.bass_isa.ReduceOp.max).then_inc(slow_all, 1)
            pool.wait_ge(feat_stored, 16)
            gathers(2, feat_rows, C)

        @block.tensor
        def _(pe):
            pe.wait_ge(s_const, CONST_ALL)
            with pe.Fori(0, W // NB) as it:
                for s in range(NB):
                    pe.wait_ge(xt_in[s], it * 16 + 16)
                    pe.wait_ge(qkv_out, (it * NB + (s - 1 if s >= 2 else s if s == 0 else 0)) * 2 + 1)
                    b = 2 * (s % 2)
                    for k in range(KC):
                        pe.matmul(px[:, b, :], xt[:, s, k, :], wqkv[:, k, 0:2 * C], start=(k == 0), stop=(k == KC - 1))
                    for k in range(KC):
                        mm = pe.matmul(px[:, b + 1, 0:C], xt[:, s, k, :], wqkv[:, k, 2 * C:3 * C], start=(k == 0), stop=(k == KC - 1))
                    mm.then_inc(xt_used, 1)
            pe.wait_ge(wtab_done, 1)

            def open_window(L, width, w):
                pe.wait_ge(opened[L], w + 1)
                pe.matmul(pa[:, 0:width], zeros[:, 0:P], zeros[:, P:P + width], start=True, stop=True, skip_group_check=True)

            pe.wait_ge(q_ready, 1)
            with pe.Fori(0, W) as w:
                first, groups, before = window(pe, w)
                open_window(0, C + H, w)
                with pe.Fori(0, groups) as k:
                    v = pe.snap(before + k)
                    for p in range(PAIRS + 1):
                        if p < PAIRS:
                            pe.wait_ge(hot[0], v * PAIRS + p + 1)
                            pe.wait_ge(hot_c[0], v * PAIRS + (2 if p >= 2 else 1))
                            for j in (2 * p, 2 * p + 1):
                                mm = pe.transpose(pt[:, p % 2, (j % 2) * P:(j % 2 + 1) * P], onehot[:, j, :], ident[:])
                            mm.then_inc(hot_t[0], 1)
                        if p >= 1:
                            q = p - 1
                            pe.wait_ge(hot_c[0], v * PAIRS + q + 2)
                            pe.wait_ge(mul1, v * PAIRS + (2 if q >= 2 else 1))
                            for j in (2 * q, 2 * q + 1):
                                for a in range(3):
                                    mm = pe.matmul(px[:, 2 * (q % 2) + j % 2, 0:C], onehot_t[:, j, :],
                                                   parts[:, bass.ds(w, 1), a, 0:C].rearrange("p o c -> p (o c)"), start=(a == 0), stop=(a == 2))
                            mm.then_inc(expd[0], 1)
                    for p in range(PAIRS):
                        pe.wait_ge(msg1, v * PAIRS + p + 1)
                        for j in (2 * p, 2 * p + 1):
                            mm = pe.matmul(pa[:, 0:C + H], onehot[:, j, :], msg[:, j, :], start=False, stop=True, skip_group_check=True)
                    mm.then_inc(summed[0], 1)
                pe.wait_ge(nv, w * NV + NVS["agg"])
                for c in range(KC):
                    mm = pe.transpose(pn[:, 0, c * P:(c + 1) * P], agg[:, c * P:(c + 1) * P], ident[:])
                mm.then_inc(nt, 1)
                pe.wait_ge(na, w * NA + NAS["aggT"])
                for c in range(KC):
                    mm = pe.matmul(pn[:, 1, 0:C], tr[:, c, :], wp[:, c, :], start=(c == 0), stop=(c == KC - 1))
                mm.then_inc(nt, 1)
                pe.wait_ge(nv, w * NV + NVS["h"])
                for c in range(KC):
                    mm = pe.transpose(pn[:, 0, c * P:(c + 1) * P], hn[:, c * P:(c + 1) * P], ident[:])
                mm.then_inc(nt, 1)
                pe.wait_ge(na, w * NA + NAS["hT"])
                for f in range(NF):
                    for c in range(KC):
                        mm = pe.matmul(px[:, f // 4, (f % 4) * P:(f % 4 + 1) * P], w1[:, c, f * P:(f + 1) * P], tr[:, c, :],
                                       start=(c == 0), stop=(c == KC - 1))
                mm.then_inc(nt, 1)
                pe.wait_ge(na, w * NA + NAS["hid"])
                for f in range(NF):
                    mm = pe.matmul(pn[:, 1, 0:C], hid[:, f, :], w2[:, f, :], start=(f == 0), stop=(f == NF - 1))
                mm.then_inc(nt, 1)
                pe.wait_ge(nv, w * NV + NVS["x1"])
                for c in range(KC):
                    mm = pe.transpose(pn[:, 0, c * P:(c + 1) * P], xs[:, c * P:(c + 1) * P], ident[:])
                mm.then_inc(nt, 1)
                pe.wait_ge(na, w * NA + NAS["x1T"])
                for c in range(KC):
                    mm = pe.matmul(px[:, 2, :], tr[:, c, :], wst[:, c, :], start=(c == 0), stop=(c == KC - 1))
                mm.then_inc(nt, 1)

            pe.wait_ge(t_ready, 1)
            with pe.Fori(0, W) as w:
                first, groups, before = window(pe, w)
                with pe.Fori(0, groups) as k:
                    v = pe.snap(before + k)
                    for p in range(PAIRS + 1):
                        if p < PAIRS:
                            pe.wait_ge(hot[1], v * PAIRS + p + 1)
                            pe.wait_ge(hot_c[1], v * PAIRS + (2 if p >= 2 else 1))
                            for j in (2 * p, 2 * p + 1):
                                mm = pe.transpose(pt[:, p % 2, (j % 2) * P:(j % 2 + 1) * P], onehot[:, j, :], ident[:])
                            mm.then_inc(hot_t[1], 1)
                        if p >= 1:
                            q = p - 1
                            pe.wait_ge(hot_c[1], v * PAIRS + q + 2)
                            pe.wait_ge(slots_free[1], v * PAIRS + PAIRS + (1 if q >= 2 else 0))
                            for j in (2 * q, 2 * q + 1):
                                for a in range(3):
                                    mm = pe.matmul(px[:, 2 * (q % 2) + j % 2, 0:CW], onehot_t[:, j, :],
                                                   parts[:, bass.ds(w, 1), a, :].rearrange("p o c -> p (o c)"), start=(a == 0), stop=(a == 2))
                            mm.then_inc(expd[1], 1)

            pe.wait_ge(ea, 1)
            pe.matmul(pn[:, 0, 0:W], zeros[:, 0:P], zeros[:, P:P + W], start=True, stop=True, skip_group_check=True)
            with pe.Fori(0, T // DT // 2) as it:
                for b in range(2):
                    pe.wait_ge(dv, it * 6 + 3 * b + 3)
                    for j in range(DT):
                        mm = pe.matmul(pn[:, 0, 0:W], lo_hot[:, b, j, :], hi_hot[:, b, j, :], start=False, stop=True, skip_group_check=True)
                    mm.then_inc(dpe, 1)

            with pe.Fori(0, W) as w:
                first, groups, before = window(pe, w)
                open_window(1, C, w)
                with pe.Fori(0, groups) as k:
                    v = pe.snap(before + k)
                    for p in range(PAIRS):
                        pe.wait_ge(hot[2], v * PAIRS + p + 1)
                        for j in (2 * p, 2 * p + 1):
                            pe.wait_ge(gathered[2][j], v * 16 + 16)
                            mm = pe.matmul(pa[:, 0:C], onehot[:, j, :], gat[:, j, 0:C], start=False, stop=True, skip_group_check=True)
                        mm.then_inc(slots_free[2], 1)
                pe.wait_ge(gv, w * GV + GVS["agg"])
                for c in range(KC):
                    mm = pe.transpose(pn[:, 0, c * P:(c + 1) * P], agg[:, c * P:(c + 1) * P], ident[:])
                mm.then_inc(gt, 1)
                pe.wait_ge(ga, w * GA + GAS["aggT"])
                for c in range(KC):
                    mm = pe.matmul(pn[:, 1, 0:C], tr[:, c, :], wfc[:, c, :], start=(c == 0), stop=(c == KC - 1))
                mm.then_inc(gt, 1)

        @block.scalar
        def _(act):
            for s in range(NB):
                act.sem_inc(kv_stored[s], 1)
            with act.Fori(0, W // NB) as it:
                for s in range(NB):
                    act.wait_ge(kv_row_ready, it * NB + s + 1)
                    act.dma_start(kv_rows[bass.ds(it * NB * P + s * P, P), :], gat[:, s, :]).then_inc(kv_stored[s], 16)
            act.wait_ge(wtab_done, 1)
            act.sem_inc(hot_c[0], 1)
            act.sem_inc(hot_c[1], 1)

            def copy_hot_t(L, v, p):
                act.wait_ge(hot_t[L], v * PAIRS + p + 1)
                act.wait_ge(expd[L], v * PAIRS + p + 1)
                act.copy(onehot_t[:, 2 * p:2 * p + 2, :], pt[:, p % 2, 0:2 * P].rearrange("p (j n) -> p j n", j=2)).then_inc(hot_c[L], 1)

            with act.Fori(0, W) as w:
                first, groups, before = window(act, w)
                with act.Fori(0, groups) as k:
                    v = act.snap(before + k)
                    for p in range(PAIRS):
                        copy_hot_t(0, v, p)
                    for p in range(PAIRS):
                        act.wait_ge(clp1, v * PAIRS + p + 1)
                        if p == 0:
                            act.wait_ge(summed[0], v + 1)
                        act.activation(msg[:, 2 * p:2 * p + 2, C:C + H], score[:, p % 2], ACT.Exp, scale=SCORE_SCALE).then_inc(exp1, 1)
                act.wait_ge(nt, w * NT + NTS["aggT"])
                act.wait_ge(nv, w * NV + NVS["agg"])
                act.copy(tr[:], pn[:, 0, 0:C].rearrange("p (k n) -> p k n", k=KC)).then_inc(na, 1)
                act.wait_ge(nv, w * NV + NVS["mv0"])
                act.activation(rstd[:, 0:1], mv[:, 1:2], ACT.Sqrt, bias=eps[:, 0:1]).then_inc(na, 1)
                act.wait_ge(nt, w * NT + NTS["hT"])
                for c in range(KC):
                    ins = act.activation(tr[:, c, :], pn[:, 0, c * P:(c + 1) * P], ACT.Identity, bias=lnb[:, c:c + 1], scale=lng[:, c:c + 1])
                ins.then_inc(na, 1)
                act.wait_ge(nt, w * NT + NTS["hid"])
                for f in range(NF):
                    ins = act.activation(hid[:, f, :], px[:, f // 4, (f % 4) * P:(f % 4 + 1) * P], ACT.Gelu, bias=b1[:, f:f + 1])
                ins.then_inc(na, 1)
                act.wait_ge(nv, w * NV + NVS["mv1"])
                act.activation(rstd[:, 0:1], mv[:, 1:2], ACT.Sqrt, bias=eps[:, 0:1]).then_inc(na, 1)
                act.wait_ge(nt, w * NT + NTS["x1T"])
                act.copy(tr[:], pn[:, 0, 0:C].rearrange("p (k n) -> p k n", k=KC)).then_inc(na, 1)
                act.copy(x1[:, bass.ds(w, 1), :].rearrange("p o c -> p (o c)"), xs[:]).then_inc(na, 1)
                act.wait_ge(nt, w * NT + NTS["proj"])
                act.copy(wide[:, bass.ds(w, 1), 0:C].rearrange("p o c -> p (o c)"), px[:, 2, C:2 * C]).then_inc(na, 1)
                act.wait_ge(proj_stored, w * 16 + 1)
                act.copy(gat_row[:, 0:C], px[:, 2, 0:C]).then_inc(na, 1)

            with act.Fori(0, W) as w:
                first, groups, before = window(act, w)
                with act.Fori(0, groups) as k:
                    v = act.snap(before + k)
                    for p in range(PAIRS):
                        copy_hot_t(1, v, p)
            act.wait_ge(ev, 6)
            act.activation(e_all[:], e_all[:], ACT.Exp, bias=shift[:, 0:1]).then_inc(ea, 1)
            with act.Fori(0, W) as w:
                act.wait_ge(gt, w * GT + GTS["aggT"])
                act.copy(tr[:], pn[:, 0, 0:C].rearrange("p (k n) -> p k n", k=KC)).then_inc(ga, 1)
                act.wait_ge(gv, w * GV + GVS["mv"])
                act.activation(rstd[:, 0:1], mv[:, 1:2], ACT.Sqrt, bias=eps[:, 0:1]).then_inc(ga, 1)

        @block.vector
        def _(dve):
            dve.memset(eps[:], EPS).then_inc(tables, 1)
            dve.memset(zeros[:], 0.0).then_inc(tables, 1)
            dve.wait_ge(s_graph, GRAPH_ALL)
            dve.wait_ge(s_const, CONST_ALL)
            dve.tensor_reduce(tile_lo[:], dst_rows, AX, ALU.min).then_inc(tables, 1)
            dve.tensor_reduce(tile_hi[:], dst_rows, AX, ALU.max).then_inc(tables, 1)
            dve.wait_ge(tables, 4)
            lo_b = tile_lo[:].unsqueeze(1).broadcast_to([P, W, TB])
            hi_b = tile_hi[:].unsqueeze(1).broadcast_to([P, W, TB])
            dve.tensor_tensor(hit2[:, 0], lo_b, tcon[:, 1], ALU.is_le).then_inc(tables, 1)
            dve.tensor_tensor(hit2[:, 1], hi_b, tcon[:, 0], ALU.is_ge).then_inc(tables, 1)
            dve.wait_ge(tables, 6)
            dve.tensor_tensor(hit[:], hit2[:, 0], hit2[:, 1], ALU.mult).then_inc(tables, 1)
            dve.wait_ge(tables, 7)
            dve.tensor_tensor(hit2[:], hit[:].unsqueeze(1).broadcast_to([P, 2, W, TB]), tcon[:, 2:4], ALU.mult).then_inc(tables, 1)
            dve.wait_ge(tables, 8)
            dve.tensor_reduce(span[:], hit2[:], AX, ALU.max).then_inc(tables, 1)
            dve.tensor_copy(dst_f[:], dst_i[:]).then_inc(tables, 1)
            dve.tensor_copy(src_f[:], src_i[:]).then_inc(tables, 1)
            dve.wait_ge(tables, 10)
            dve.tensor_scalar(dst_i[:], src_i[:], 7, None, ALU.arith_shift_right).then_inc(tables, 1)
            dve.wait_ge(tables, 12)
            dve.tensor_copy(src_hi[:], dst_i[:]).then_inc(tables, 1)
            dve.wait_ge(tables, 13)
            dve.scalar_tensor_tensor(out=src_lo[:], in0=src_hi[:], scalar=float(-P), in1=src_f[:], op0=ALU.mult, op1=ALU.add).then_inc(tables, 1)
            dve.tensor_scalar(attn_lo[:], attn[:], SLOPE, None, ALU.mult).then_inc(tables, 1)
            dve.tensor_scalar(attn_hi[:], attn[:], 1.0 - SLOPE, None, ALU.mult).then_inc(tables, 1)
            dve.memset(e_all[:], 0.0).then_inc(tables, 1)
            dve.memset(wide[:, :, C + 1:C + 2], 1.0).then_inc(tables, 1)
            n = 18
            dve.wait_ge(span_red, 1)
            end, start = span_all[0:1, 0, :], span_all[0:1, 1, :]

            def link(ins):
                nonlocal n
                n += 1
                ins.then_inc(tables, 1)
                dve.wait_ge(tables, n)

            link(dve.tensor_scalar(wf[:, 0], start, -1.0, float(TPAD), ALU.mult, ALU.add))
            link(dve.tensor_scalar(wf[:, 0], wf[:, 0], float(T - 1), None, ALU.min))
            link(dve.tensor_tensor(wf[:, 1], end, wf[:, 0], ALU.subtract))
            link(dve.tensor_scalar(wf[:, 1], wf[:, 1], float(G - 1), float(G), ALU.add, ALU.max))
            link(dve.tensor_scalar(wf[:, 1], wf[:, 1], 1.0 / G, -0.5 + 0.5 / G, ALU.mult, ALU.add))
            link(dve.tensor_scalar(wf[:, 1], wf[:, 1], 8388608.0, None, ALU.add))
            link(dve.tensor_scalar(wf[:, 1], wf[:, 1], -8388608.0, None, ALU.add))
            link(dve.memset(wf[:, 3], 0.0))
            link(dve.tensor_tensor_scan(wf[:, 2], wf[:, 1], wf[:, 3], 0.0, ALU.add, ALU.add))
            link(dve.tensor_tensor(wf[:, 2], wf[:, 2], wf[:, 1], ALU.subtract))
            link(dve.tensor_copy(wtab[:].rearrange("o (w a) -> o a w", a=4)[:, 0:3], wf[:, 0:3]))
            dve.sem_inc(wtab_done, 1)

            dve.sem_inc(qkv_out, 1)
            with dve.Fori(0, W // NB) as it:
                for s in range(NB):
                    b = 2 * (s % 2)
                    dve.wait_ge(xt_used, it * NB + s + 2)
                    dve.wait_ge(kv_stored[s], it * 16 + 1)
                    dve.tensor_tensor(gat[:, s, :], px[:, b, :], bqkv[:, 0:2 * C], ALU.add).then_inc(kv_row_ready, 1)
                    dve.wait_ge(kv_row_ready, it * NB + s + 1)
                    dve.sem_inc(qkv_out, 1)
                    dve.tensor_tensor(wide[:, bass.ds(it * NB + s, 1), 0:C].rearrange("p o c -> p (o c)"), px[:, b + 1, 0:C], bqkv[:, 2 * C:3 * C], ALU.add).then_inc(qkv_out, 1)

            def split(width, base):
                m = base
                for a in range(3):
                    dve.tensor_copy(parts[:, :, a, 0:width], wide[:, :, 0:width]).then_inc(split_v, 1)
                    m += 1
                    dve.wait_ge(split_v, m)
                    if a < 2:
                        dve.tensor_tensor(wide[:, :, 0:width], wide[:, :, 0:width], parts[:, :, a, 0:width], ALU.subtract).then_inc(split_v, 1)
                        m += 1
                        dve.wait_ge(split_v, m)
                return m

            dve.wait_ge(qkv_out, 2 * W + 1)
            m = split(C, 0)
            dve.sem_inc(q_ready, 1)

            def group_hots(L, w, v, t0):
                if L == 0:
                    dve.wait_ge(summed[0], v + 1)
                else:
                    dve.wait_ge(expd[1], v * PAIRS + PAIRS)
                dve.tensor_scalar(dst_g[:], dst_f[:, bass.ds(t0, G)], wlo[:, bass.ds(w, 1)], None, ALU.subtract).then_inc(gdst[L], 1)
                dve.wait_ge(gdst[L], v + 1)
                for p in range(PAIRS):
                    dve.tensor_tensor(onehot[:, 2 * p:2 * p + 2, :], iota[:].unsqueeze(1).broadcast_to([P, 2, P]),
                                      dst_g[:, 2 * p:2 * p + 2].unsqueeze(2).broadcast_to([P, 2, P]), ALU.is_equal).then_inc(hot[L], 1)

            dve.sem_inc(summed[0], 1)
            dve.sem_inc(opened[0], 1)
            dve.sem_inc(mul1, 1)
            dve.sem_inc(slots_free[0], PAIRS)
            dve.sem_inc(expd[0], PAIRS)
            dve.sem_inc(expd[1], PAIRS)
            dve.sem_inc(proj_stored, 1)
            with dve.Fori(0, W) as w:
                first, groups, before = window(dve, w)
                with dve.Fori(0, groups) as k:
                    v = dve.snap(before + k)
                    t0 = first_tile(first, k)
                    group_hots(0, w, v, t0)
                    for p in range(PAIRS + 1):
                        if p < PAIRS:
                            b = 2 * (p % 2)
                            dve.wait_ge(expd[0], v * PAIRS + p + 1 + PAIRS)
                            for j in (2 * p, 2 * p + 1):
                                dve.wait_ge(gathered[0][j], v * 16 + 16)
                            dve.tensor_tensor(prod[:, p % 2, 0:2 * C].rearrange("p (j c) -> p j c", j=2), px[:, b:b + 2, 0:C],
                                              gat[:, 2 * p:2 * p + 2, 0:C], ALU.mult).then_inc(mul1, 1)
                        if p >= 1:
                            q = p - 1
                            dve.wait_ge(exp1, v * PAIRS + q + 1)
                            dve.tensor_tensor(msg[:, 2 * q:2 * q + 2, 0:C].rearrange("p j (h d) -> p j h d", h=H),
                                              gat[:, 2 * q:2 * q + 2, C:2 * C].rearrange("p j (h d) -> p j h d", h=H),
                                              msg[:, 2 * q:2 * q + 2, C:C + H].unsqueeze(3).broadcast_to([P, 2, H, HD]),
                                              ALU.mult).then_inc(msg1, 1)
                            dve.wait_ge(msg1, v * PAIRS + q + 1)
                            dve.sem_inc(slots_free[0], 1)
                        if p < PAIRS:
                            dve.wait_ge(mul1, v * PAIRS + p + 2)
                            dve.tensor_reduce(score[:, p % 2], prod[:, p % 2, 0:2 * C].rearrange("p (j h d) -> p j h d", j=2, h=H), AX, ALU.add).then_inc(red1, 1)
                            dve.wait_ge(red1, v * PAIRS + p + 1)
                            dve.tensor_scalar(score[:, p % 2], score[:, p % 2], CLIP, -CLIP, ALU.min, ALU.max).then_inc(clp1, 1)
                dve.wait_ge(summed[0], before + groups + 1)

                def at(name):
                    return w * NV + NVS[name]

                dve.tensor_scalar(den[:, 0], pa[:, C:C + H], 0.0, None, ALU.is_equal).then_inc(nv, 1)
                dve.wait_ge(nv, at("den0"))
                dve.tensor_tensor(den[:, 1], den[:, 0], pa[:, C:C + H], ALU.add).then_inc(nv, 1)
                dve.wait_ge(nv, at("den1"))
                dve.reciprocal(den[:, 2], den[:, 1]).then_inc(nv, 1)
                dve.wait_ge(nv, at("den2"))
                dve.tensor_tensor(agg[:].rearrange("p (h d) -> p h d", h=H), pa[:, 0:C].rearrange("p (h d) -> p h d", h=H),
                                  den[:, 2].unsqueeze(2).broadcast_to([P, H, HD]), ALU.mult).then_inc(nv, 1)
                dve.wait_ge(nv, at("agg"))
                dve.wait_ge(x_in, w * 16 + 16)
                dve.wait_ge(nt, w * NT + NTS["y"])
                dve.tensor_tensor(xm[:], pn[:, 1, 0:C], bp[:], ALU.add).then_inc(nv, 1)
                dve.wait_ge(nv, at("xm0"))
                dve.tensor_tensor(xm[:], xm[:], x_w[:], ALU.add).then_inc(nv, 1)
                dve.wait_ge(nv, at("xm1"))
                dve.bn_stats(stats[:], xm[:]).then_inc(nv, 1)
                dve.wait_ge(nv, at("st0"))
                dve.sem_inc(dve_seen, 1)
                dve.bn_aggr(mv[:], stats[:]).then_inc(nv, 1)
                dve.wait_ge(na, w * NA + 2)
                dve.reciprocal(rstd[:, 1:2], rstd[:, 0:1]).then_inc(nv, 1)
                dve.wait_ge(nv, at("rs0"))
                dve.tensor_scalar(hn[:], xm[:], mv[:, 0:1], rstd[:, 1:2], ALU.subtract, ALU.mult).then_inc(nv, 1)
                dve.wait_ge(nt, w * NT + NTS["mlp"])
                dve.tensor_tensor(xs[:], pn[:, 1, 0:C], b2[:], ALU.add).then_inc(nv, 1)
                dve.wait_ge(nv, at("xs0"))
                dve.tensor_tensor(xs[:], xs[:], xm[:], ALU.add).then_inc(nv, 1)
                dve.wait_ge(nv, at("xs1"))
                dve.tensor_tensor(xs[:], xs[:], x_w[:], ALU.add).then_inc(nv, 1)
                dve.wait_ge(nv, at("xs2"))
                dve.bn_stats(stats[:], xs[:]).then_inc(nv, 1)
                dve.wait_ge(nv, at("st1"))
                dve.sem_inc(dve_seen, 1)
                dve.bn_aggr(mv[:], stats[:]).then_inc(nv, 1)
                dve.wait_ge(na, w * NA + 5)
                dve.reciprocal(rstd[:, 1:2], rstd[:, 0:1]).then_inc(nv, 1)
                dve.wait_ge(nv, at("rs1"))
                dve.tensor_scalar(xs[:], xs[:], mv[:, 0:1], rstd[:, 1:2], ALU.subtract, ALU.mult).then_inc(nv, 1)
                dve.wait_ge(na, w * NA + NAS["proj_row"])
                dve.wait_ge(proj_stored, w * 16 + 1)
                dve.scalar_tensor_tensor(out=prod[:, 0, 0:C], in0=px[:, 2, 0:C], scalar=1.0, in1=attn_lo[:], op0=ALU.mult, op1=ALU.mult,
                                         accum_out=gat_row[:, C:C + 1]).then_inc(nv, 1)
                dve.scalar_tensor_tensor(out=prod[:, 1, 0:C], in0=px[:, 2, C:2 * C], scalar=1.0, in1=attn_lo[:], op0=ALU.mult, op1=ALU.mult,
                                         accum_out=wide[:, bass.ds(w, 1), C:C + 1].rearrange("p o c -> p (o c)")).then_inc(nv, 1)
                dve.memset(gat_row[:, C + 1:C + 2], 0.0).then_inc(nv, 1)
                dve.wait_ge(nv, at("proj_row"))
                dve.wait_ge(na, w * NA + NA)
                dve.sem_inc(opened[0], 1)

            dve.wait_ge(nv, W * NV)
            dve.wait_ge(na, W * NA)
            m = split(CW, m)
            dve.sem_inc(t_ready, 1)
            dve.sem_inc(slots_free[1], PAIRS)
            ZSTEPS = PAIRS + G + 4
            with dve.Fori(0, W) as w:
                first, groups, before = window(dve, w)
                with dve.Fori(0, groups) as k:
                    v = dve.snap(before + k)
                    t0 = first_tile(first, k)
                    group_hots(1, w, v, t0)
                    for p in range(PAIRS):
                        b = 2 * (p % 2)
                        dve.wait_ge(expd[1], v * PAIRS + p + 1 + PAIRS)
                        for j in (2 * p, 2 * p + 1):
                            dve.wait_ge(gathered[1][j], v * 16 + 16)
                        dve.tensor_tensor(zbuf[:, 2 * p:2 * p + 2, :], px[:, b:b + 2, 0:CW], gat[:, 2 * p:2 * p + 2, 0:CW], ALU.add).then_inc(zs, 1)
                        dve.wait_ge(zs, v * ZSTEPS + p * 3 + 1)
                        dve.sem_inc(slots_free[1], 1)
                        for j in (2 * p, 2 * p + 1):
                            dve.scalar_tensor_tensor(out=prod[:, j % 2, 0:C], in0=zbuf[:, j, 0:C], scalar=0.0, in1=attn_hi[:],
                                                     op0=ALU.max, op1=ALU.mult, accum_out=dots[:, 0, j:j + 1]).then_inc(zs, 1)
                    dve.wait_ge(zs, v * ZSTEPS + PAIRS + G)
                    dve.tensor_tensor(dots[:, 1], dots[:, 0], zbuf[:, :, C], ALU.add).then_inc(zs, 1)
                    dve.wait_ge(zs, v * ZSTEPS + PAIRS + G + 1)
                    dve.tensor_tensor(dots[:, 2], dots[:, 1], zbuf[:, :, C + 1], ALU.mult).then_inc(zs, 1)
                    dve.wait_ge(zs, v * ZSTEPS + PAIRS + G + 2)
                    dve.tensor_tensor(e_all[:, bass.ds(t0, G)], e_all[:, bass.ds(t0, G)], dots[:, 2], ALU.add).then_inc(zs, 1)
                    dve.wait_ge(zs, v * ZSTEPS + PAIRS + G + 3)
                    dve.sem_inc(zs, 1)

            dve.memset(e_all[:, T:TPAD], -FAR).then_inc(sv, 1)
            dve.tensor_reduce(rng[:, 0:1], e_all[:, 0:T], AX, ALU.max).then_inc(ev, 1)
            dve.tensor_reduce(dots[:, 0, 0:1], e_all[:, 0:T], AX, ALU.min).then_inc(sv, 1)
            dve.wait_ge(sv, 2)
            dve.tensor_scalar(rng[:, 1:2], dots[:, 0, 0:1], -1.0, None, ALU.mult).then_inc(ev, 1)
            dve.wait_ge(ep, 1)
            dve.tensor_tensor(dots[:, 1, 0:1], rng_all[:, 0:1], rng_all[:, 1:2], ALU.add).then_inc(ev, 1)
            dve.wait_ge(ev, 3)
            dve.tensor_scalar(slow_i[:], dots[0:1, 1, 0:1], SPREAD, None, ALU.is_gt).then_inc(ev, 1)
            dve.tensor_scalar(shift[:], rng_all[:, 0:1], -1.0, None, ALU.mult).then_inc(ev, 1)
            dve.wait_ge(ev, 5)
            dve.sem_inc(slow_flag, 1)
            slow = dve.alloc_register("slow_dve")
            dve.reg_load(slow, slow_i[0:1, 0:1])
            count, pen, masked, m_edge = dots[:, 2, 0:1], gat[:, 0:2].rearrange("p j c -> p (j c)")[:, 0:T], \
                gat[:, 2:4].rearrange("p j c -> p (j c)")[:, 0:T], gat[:, 4:6].rearrange("p j c -> p (j c)")[:, 0:T]
            with dve.If_ne(slow, 0):
                dve.memset(count, 0.0).then_inc(sv, 1)
                dve.memset(m_edge, 0.0).then_inc(sv, 1)
                with dve.Fori(0, NP) as node:
                    dve.wait_ge(sv, node * 4 + 4)
                    dve.tensor_scalar(pen, src_f[:, 0:T], count, -FAR, ALU.not_equal, ALU.mult).then_inc(sv, 1)
                    dve.wait_ge(sv, node * 4 + 5)
                    dve.tensor_tensor(masked, e_all[:, 0:T], pen, ALU.add).then_inc(sv, 1)
                    dve.wait_ge(sv, node * 4 + 6)
                    dve.tensor_reduce(node_max[:, bass.ds(node, 1)], masked, AX, ALU.max).then_inc(sv, 1)
                    dve.wait_ge(sv, node * 4 + 7)
                    dve.tensor_scalar(count, count, 1.0, None, ALU.add).then_inc(sv, 1)
                dve.wait_ge(sv, NP * 4 + 4)
                dve.sem_inc(slow_max, 1)
                dve.wait_ge(slow_all, 1)
                dve.memset(count, 0.0).then_inc(sv, 1)
                with dve.Fori(0, NP) as node:
                    dve.wait_ge(sv, node * 3 + NP * 4 + 5)
                    dve.tensor_scalar(pen, src_f[:, 0:T], count, node_max_all[:, bass.ds(node, 1)], ALU.is_equal, ALU.mult).then_inc(sv, 1)
                    dve.wait_ge(sv, node * 3 + NP * 4 + 6)
                    dve.tensor_tensor(m_edge, m_edge, pen, ALU.add).then_inc(sv, 1)
                    dve.wait_ge(sv, node * 3 + NP * 4 + 7)
                    dve.tensor_scalar(count, count, 1.0, None, ALU.add).then_inc(sv, 1)
                dve.wait_ge(sv, NP * 7 + 5)
                dve.tensor_tensor(e_all[:, 0:T], e_all[:, 0:T], m_edge, ALU.subtract).then_inc(sv, 1)
                dve.memset(shift[:], 0.0).then_inc(sv, 1)
                dve.wait_ge(sv, NP * 7 + 7)
            dve.sem_inc(ev, 1)

            dve.wait_ge(ea, 1)
            dve.sem_inc(dpe, 2)
            with dve.Fori(0, T // DT // 2) as it:
                for b in range(2):
                    dve.wait_ge(dpe, it * 2 + b + 1)
                    t0 = it * 2 * DT + b * DT
                    dve.tensor_tensor(lo_hot[:, b], iota[:].unsqueeze(1).broadcast_to([P, DT, P]),
                                      src_lo[:, bass.ds(t0, DT)].unsqueeze(2).broadcast_to([P, DT, P]), ALU.is_equal).then_inc(dv, 1)
                    dve.tensor_tensor(hi_hot[:, b], iota[:, 0:W].unsqueeze(1).broadcast_to([P, DT, W]),
                                      src_hi[:, bass.ds(t0, DT)].unsqueeze(2).broadcast_to([P, DT, W]), ALU.is_equal).then_inc(dv, 1)
                    dve.wait_ge(dv, it * 6 + 3 * b + 2)
                    dve.tensor_tensor(hi_hot[:, b], hi_hot[:, b],
                                      e_all[:, bass.ds(t0, DT)].unsqueeze(2).broadcast_to([P, DT, W]), ALU.mult).then_inc(dv, 1)
            dve.wait_ge(dpe, T // DT + 2)
            dve.tensor_scalar(denom[:, 0], pn[:, 0, 0:W], 0.0, None, ALU.is_equal).then_inc(fv, 1)
            dve.wait_ge(fv, 1)
            dve.tensor_tensor(denom[:, 1], denom[:, 0], pn[:, 0, 0:W], ALU.add).then_inc(fv, 1)
            dve.wait_ge(fv, 2)
            dve.reciprocal(denom[:, 2], denom[:, 1]).then_inc(fv, 1)
            dve.wait_ge(fv, 3)
            dve.tensor_tensor(feats, x1[:], denom[:, 2].unsqueeze(2).broadcast_to([P, W, C]), ALU.mult).then_inc(fv, 1)

            dve.sem_inc(opened[1], 1)
            dve.sem_inc(slots_free[2], PAIRS)
            dve.sem_inc(out_stored, 1)
            with dve.Fori(0, W) as w:
                first, groups, before = window(dve, w)
                with dve.Fori(0, groups) as k:
                    v = dve.snap(before + k)
                    t0 = first_tile(first, k)
                    dve.tensor_scalar(dst_g[:], dst_f[:, bass.ds(t0, G)], wlo[:, bass.ds(w, 1)], None, ALU.subtract).then_inc(gdst[2], 1)
                    dve.tensor_copy(ex_g[:], e_all[:, bass.ds(t0, G)]).then_inc(gdst[2], 1)
                    dve.wait_ge(gdst[2], v * 2 + 2)
                    for p in range(PAIRS):
                        dve.wait_ge(slots_free[2], v * PAIRS + p + 1)
                        for j in (2 * p, 2 * p + 1):
                            ins = dve.tensor_scalar(onehot[:, j, :], iota[:], dst_g[:, j:j + 1], ex_g[:, j:j + 1], ALU.is_equal, ALU.mult)
                        ins.then_inc(hot[2], 1)
                    dve.wait_ge(hot[2], v * PAIRS + PAIRS)
                dve.wait_ge(slots_free[2], (before + groups) * PAIRS + PAIRS)

                def at(name):
                    return w * GV + GVS[name]

                dve.tensor_copy(agg[:], pa[:, 0:C]).then_inc(gv, 1)
                dve.wait_ge(gv, at("agg"))
                dve.sem_inc(opened[1], 1)
                dve.wait_ge(gt, w * GT + GTS["y"])
                dve.tensor_tensor(xm[:], pn[:, 1, 0:C], bfc[:], ALU.add).then_inc(gv, 1)
                dve.wait_ge(gv, at("y0"))
                dve.tensor_tensor(xm[:], xm[:], x1[:, bass.ds(w, 1), :].rearrange("p o c -> p (o c)"), ALU.add).then_inc(gv, 1)
                dve.wait_ge(gv, at("y1"))
                dve.bn_stats(stats[:], xm[:]).then_inc(gv, 1)
                dve.wait_ge(gv, at("st"))
                dve.sem_inc(dve_seen, 1)
                dve.bn_aggr(mv[:], stats[:]).then_inc(gv, 1)
                dve.wait_ge(ga, w * GA + GAS["sqrt"])
                dve.reciprocal(rstd[:, 1:2], rstd[:, 0:1]).then_inc(gv, 1)
                dve.wait_ge(gv, at("rs"))
                dve.wait_ge(out_stored, w * 16 + 1)
                dve.tensor_scalar(hn[:], xm[:], mv[:, 0:1], rstd[:, 1:2], ALU.subtract, ALU.mult).then_inc(gv, 1)


INPUTS = ["src", "dst", "dst_r", "x", "xt", "wqkv", "bqkv", "wp", "bp", "lng", "lnb", "w1", "b1", "w2", "b2",
          "wst", "attn", "wfc", "bfc", "c_iota", "c_ident", "c_wlo", "c_tcon"]


def shape_constants():
    window = np.arange(W, dtype=np.float32) * P
    tile = (np.arange(TB)[None, :] * P + np.arange(P)[:, None]).astype(np.float32)
    grid = np.empty((P, 4, W, TB), np.float32)
    grid[:, 0] = window[None, :, None]
    grid[:, 1] = window[None, :, None] + (P - 1)
    grid[:, 2] = tile[:, None, :] + 1
    grid[:, 3] = TPAD - tile[:, None, :]
    grid[:, 2:] *= tile[:, None, None, :] < T
    return {
        "c_iota": np.broadcast_to(np.arange(P, dtype=np.float32), (P, P)).copy(),
        "c_ident": np.eye(P, dtype=np.float32),
        "c_wlo": np.broadcast_to(window, (P, W)).copy(),
        "c_tcon": grid,
    }


def kernel(x, src, dst, L0_gnn_Wq, L0_gnn_bq, L0_gnn_Wk, L0_gnn_bk, L0_gnn_Wv, L0_gnn_bv, L0_gnn_Wp, L0_gnn_bp,
           L0_gnn_ln_g, L0_gnn_ln_b, L0_gnn_W1, L0_gnn_b1, L0_gnn_W2, L0_gnn_b2,
           L1_gnn_W_s, L1_gnn_W_t, L1_gnn_W_attn, L1_gnn_W_fc, L1_gnn_b_fc):
    import concourse.bacc as bacc
    from concourse.bass_utils import run_bass_kernel_spmd

    a = {k: np.asarray(v) for k, v in locals().items() if k not in ("bacc", "run_bass_kernel_spmd")}
    x = np.zeros((NP, C), a["x"].dtype)
    x[:N_NODES] = a["x"]

    def edges(e):
        out = np.full((TPAD * P,), FAKE, e.dtype)
        out[:N_EDGES] = e
        return out.reshape(TPAD, P)

    def columns(v):
        return v.reshape(-1, P).T

    arrays = {
        "src": edges(a["src"]).T, "dst": edges(a["dst"]).T, "dst_r": edges(a["dst"]),
        "x": x, "xt": x.reshape(W, P, KC, P).transpose(0, 3, 2, 1),
        "wqkv": np.concatenate([a["L0_gnn_Wk"].T, a["L0_gnn_Wv"].T, a["L0_gnn_Wq"].T], axis=1),
        "bqkv": np.concatenate([a["L0_gnn_bk"], a["L0_gnn_bv"], a["L0_gnn_bq"]]),
        "wp": a["L0_gnn_Wp"].T, "bp": a["L0_gnn_bp"],
        "lng": columns(a["L0_gnn_ln_g"]), "lnb": columns(a["L0_gnn_ln_b"]),
        "w1": a["L0_gnn_W1"].T, "b1": columns(a["L0_gnn_b1"]), "w2": a["L0_gnn_W2"].T, "b2": a["L0_gnn_b2"],
        "wst": np.concatenate([a["L1_gnn_W_s"].T, a["L1_gnn_W_t"].T], axis=1),
        "attn": a["L1_gnn_W_attn"].reshape(C), "wfc": a["L1_gnn_W_fc"].T, "bfc": a["L1_gnn_b_fc"],
    }
    arrays.update(shape_constants())
    arrays = {f"in_{k}": np.ascontiguousarray(arrays[k]) for k in INPUTS}

    nc = bacc.Bacc("TRN2", target_bir_lowering=False, num_devices=1)
    io = {k: nc.dram_tensor(f"in_{k}", arrays[f"in_{k}"].shape, mybir.dt.from_np(arrays[f"in_{k}"].dtype), kind="ExternalInput").ap()
          for k in INPUTS}
    io["out"] = nc.dram_tensor("out", (N_NODES, C), F32, kind="ExternalOutput").ap()
    build(nc, io)
    return run_bass_kernel_spmd(nc, [arrays], core_ids=[0]).results[0]["out"]
```

```python
from contextlib import ExitStack

import numpy as np

import concourse.bass as bass
from concourse import mybir

ALU = mybir.AluOpType
ACT = mybir.ActivationFunctionType
AX = mybir.AxisListType.X
F32 = mybir.dt.float32
BF16 = mybir.dt.bfloat16
I32 = mybir.dt.int32

P = 128
N_NODES = 3125
C = 256
H = 8
HD = C // H
FF = 4 * C
KC = C // P
NF = FF // P
E_DRAWN = 50000
N_EDGES = 2 * E_DRAWN + N_NODES
W = -(-N_NODES // P)
NP = W * P
FAKE = NP - 1
T = -(-N_EDGES // P)
TB = -(-T // P)
TPAD = TB * P
G = 6
PAIRS = G // 2
CW = C + 2
DT = 13
WCOLS = 5
NB = 5
EPS = 1e-5
SLOPE = 0.2
CLIP = 10.0 * float(HD) ** 0.5
SCORE_SCALE = 1.0 / float(HD) ** 0.5
FAR = 3.0e38
SPREAD = 60.0
assert T % DT == 0 and W % NB == 0 and TPAD >= T + G


def build(nc, io):
    ctx = ExitStack()
    with ctx:
        def sb(name, shape, dt=F32):
            return ctx.enter_context(nc.sbuf_tensor("sb_" + name, shape, dt))

        def psum(name, shape, dt=F32):
            return ctx.enter_context(nc.psum_tensor("ps_" + name, shape, dt))

        def sem(name):
            return ctx.enter_context(nc.semaphore(name))

        def dram(name, shape, dt=F32):
            return nc.dram_tensor(name, shape, dt, kind="Internal").ap()

        kv_rows = dram("kv_rows", [NP, 2 * C])
        proj_rows = dram("proj_rows", [NP, CW])
        feat_rows = dram("feat_rows", [NP, C])

        iota = sb("iota", [P, P])
        iota_b = sb("iota_b", [P, P], BF16)
        iota_w = sb("iota_w", [P, P])
        nnode = sb("nnode", [P, W])
        pick = sb("pick", [3 * W, W])
        ident = sb("ident", [P, P])
        wlo = sb("wlo", [P, W])
        zeros = sb("zeros", [1, P + 2 * C])
        wqkv = sb("wqkv", [P, KC, 3 * C])
        wp = sb("wp", [P, KC, C])
        w1 = sb("w1", [P, KC, FF])
        w2 = sb("w2", [P, NF, C])
        wst = sb("wst", [P, KC, 2 * C])
        wfc = sb("wfc", [P, KC, C])
        bqkv = sb("bqkv", [P, 3 * C])
        bp = sb("bp", [P, C])
        b1 = sb("b1", [P, NF])
        b2 = sb("b2", [P, C])
        bfc = sb("bfc", [P, C])
        lng = sb("lng", [P, KC])
        lnb = sb("lnb", [P, KC])
        attn = sb("attn", [P, C])
        attn_lo = sb("attn_lo", [P, C])
        attn_hi = sb("attn_hi", [P, C])
        eps = sb("eps", [P, 1])

        ndst_f = sb("ndst_f", [P, TPAD])
        src_f = sb("src_f", [P, TPAD])
        src_hib = sb("src_hib", [P, TPAD], BF16)
        src_lob = sb("src_lob", [P, TPAD], BF16)
        e_all = sb("e_all", [P, TPAD])

        x1 = sb("x1", [P, W, C])
        wide = sb("wide", [P, W, CW])
        parts = sb("parts", [P, W, 3, CW], BF16)

        early = x1[:].rearrange("p w c -> p (w c)")
        dst_rows = early[:, 0:TPAD].bitcast(I32).rearrange("p (b e) -> p b e", b=TB)
        src_i = early[:, TPAD:2 * TPAD].bitcast(I32)
        dst_i = early[:, 2 * TPAD:3 * TPAD].bitcast(I32)
        src_hi = early[:, 3 * TPAD:4 * TPAD]
        tcon_at, grid = 4 * TPAD, W * TB
        tcon = early[:, tcon_at:tcon_at + 4 * grid].rearrange("p (a w b) -> p a w b", a=4, w=W)
        hit = early[:, tcon_at + 4 * grid:tcon_at + 5 * grid].rearrange("p (w b) -> p w b", w=W)
        hit2 = early[:, tcon_at + 5 * grid:tcon_at + 7 * grid].rearrange("p (a w b) -> p a w b", a=2, w=W)

        tile_lo = sb("tile_lo", [P, TB])
        tile_hi = sb("tile_hi", [P, TB])
        span = sb("span", [P, 2, W])
        span_all = sb("span_all", [P, 2, W])
        wf = sb("wf", [1, 5, W])
        wtab = sb("wtab", [1, WCOLS * W], I32)

        gat = sb("gat", [P, G, 2 * C])
        idx = sb("idx", [P, G], I32)
        drow = sb("drow", [P, G, P], I32)
        away_t = sb("away_t", [P, G, P], BF16)
        away = sb("away", [P, G, P], BF16)
        dst_g = sb("dst_g", [P, G])
        ex_g = sb("ex_g", [P, G])
        onehot = sb("onehot", [P, G, P])
        onehot_t = sb("onehot_t", [P, G, P], BF16)
        prod = sb("prod", [P, 2, 2 * C])
        score = sb("score", [P, PAIRS, 2, H])
        msg = sb("msg", [P, G, C + H])
        zbuf = msg[:, :, 0:CW]
        e_parts = msg[:].rearrange("p j c -> p (j c)").bitcast(BF16)[:, 0:3 * T].rearrange("p (a t) -> p a t", a=3)
        dots = sb("dots", [P, 3, G])

        den = sb("den", [P, 3, H])
        agg = sb("agg", [P, C])
        xw = sb("xw", [P, NB, C])
        xm = sb("xm", [P, NB, C])
        xs = msg[:].rearrange("p j c -> p (j c)")[:, 0:NB * C].rearrange("p (s c) -> p s c", s=NB)
        hn = sb("hn", [P, NB, C])
        tr = sb("tr", [P, NB, KC, P])
        xt = tr
        hid = gat[:, 0:4, :].rearrange("p (b f) n -> p b (f n)", b=2).rearrange("p b (f n) -> p b f n", n=P)
        row = wqkv[:].rearrange("p k n -> p (k n)")[:, 0:NB * CW].rearrange("p (s c) -> p s c", s=NB)
        stats = sb("stats", [P, NB, 6])
        mv = sb("mv", [P, NB, 2])
        rstd = sb("rstd", [P, 2, NB])
        denom = sb("denom", [P, 3, W])
        d75 = sb("d75", [3 * W, P])
        rng = sb("rng", [P, 2])
        rng_all = sb("rng_all", [P, 2])
        shift = sb("shift", [P, 1])
        slow_i = sb("slow_i", [1, 1], I32)

        px = psum("px", [P, 6, 512])
        pa = psum("pa", [P, 512])
        pn = psum("pn", [P, 512])

        s_const = sem("s_const")
        s_graph = sem("s_graph")
        block = ctx.enter_context(nc.Block())

        tables = sem("tables")
        span_red = sem("span_red")
        wtab_done = sem("wtab_done")
        xt_in = [sem(f"xt_in{s}") for s in range(NB)]
        xt_used = sem("xt_used")
        qkv_out = sem("qkv_out")
        kv_row_ready = sem("kv_row_ready")
        kv_stored = [sem(f"kv_stored{s}") for s in range(NB)]
        split_v = sem("split_v")
        q_ready = sem("q_ready")
        gathered = [[sem(f"gathered{L}_{j}") for j in range(G)] for L in range(3)]
        idx_in = [[sem(f"idx_in{L}_{p}") for p in range(PAIRS)] for L in range(3)]
        pool_seen = sem("pool_seen")
        slots_free = [sem(f"slots_free{L}") for L in range(3)]
        drow_in = [sem(f"drow_in{L}") for L in range(2)]
        far = [sem(f"far{L}") for L in range(2)]
        far_e = sem("far_e")
        iotaw_set = sem("iotaw_set")
        hot_t = [sem(f"hot_t{L}") for L in range(2)]
        hot = [sem(f"hot{L}") for L in (0, 1)]
        expd = [sem(f"expd{L}") for L in range(2)]
        dgs = sem("dgs")
        mul1 = sem("mul1")
        red1 = sem("red1")
        clp1 = sem("clp1")
        exp1 = sem("exp1")
        msg1 = sem("msg1")
        summed = sem("summed")
        opened = [sem(f"opened{L}") for L in (0, 1)]
        nd = sem("nd")
        xw_in = sem("xw_in")
        nv = sem("nv")
        na = sem("na")
        nt = sem("nt")
        npl = sem("npl")
        proj_stored = sem("proj_stored")
        t_ready = sem("t_ready")
        zs = sem("zs")
        ev = sem("ev")
        ea = sem("ea")
        ep = sem("ep")
        slow_flag = sem("slow_flag")
        sv = sem("sv")
        slow_max = sem("slow_max")
        slow_all = sem("slow_all")
        dv = sem("dv")
        dpe = sem("dpe")
        fv = sem("fv")
        fpe = sem("fpe")
        dsplit = sem("dsplit")
        sp_seen, act_seen = sem("sp_seen"), sem("act_seen")
        dve_seen = sem("dve_seen")
        feat_stored = sem("feat_stored")
        gv = sem("gv")
        ga = sem("ga")
        gt = sem("gt")
        out_stored = sem("out_stored")

        CONSTS = [
            (wqkv[:], io["wqkv"].rearrange("(k p) n -> p k n", p=P)),
            (bqkv[:], io["bqkv"].partition_broadcast(P)),
            (iota[:], io["c_iota"]), (ident[:], io["c_ident"]), (wlo[:], io["c_wlo"]), (nnode[:], io["c_nnode"]),
            (pick[:], io["c_pick"]), (tcon[:], io["c_tcon"]),
            (wp[:], io["wp"].rearrange("(k p) n -> p k n", p=P)),
            (w1[:], io["w1"].rearrange("(k p) n -> p k n", p=P)),
            (w2[:], io["w2"].rearrange("(k p) n -> p k n", p=P)),
            (wst[:], io["wst"].rearrange("(k p) n -> p k n", p=P)),
            (wfc[:], io["wfc"].rearrange("(k p) n -> p k n", p=P)),
            (bp[:], io["bp"].partition_broadcast(P)),
            (b1[:], io["b1"]), (b2[:], io["b2"].partition_broadcast(P)),
            (bfc[:], io["bfc"].partition_broadcast(P)), (lng[:], io["lng"]), (lnb[:], io["lnb"]),
            (attn[:], io["attn"].partition_broadcast(P)),
        ]
        GRAPH = [(src_i[:], io["src"]), (dst_i[:], io["dst"]), (dst_rows, io["dst_r"].rearrange("(b p) e -> p b e", p=P))]
        CONST_ALL = 16 * len(CONSTS)
        GRAPH_ALL = 16 * len(GRAPH)

        def window(eng, w):
            most = -(-T // G) + 1
            first = eng.value_load(wtab[0:1, bass.ds(w * WCOLS, 1)], min_val=0, max_val=T - 1)
            groups = eng.value_load(wtab[0:1, bass.ds(w * WCOLS + 1, 1)], min_val=2, max_val=most)
            before = eng.value_load(wtab[0:1, bass.ds(w * WCOLS + 2, 1)], min_val=0, max_val=W * most)
            return first, groups, before

        def last_group(eng, w):
            return eng.value_load(wtab[0:1, bass.ds(w * WCOLS + 3, 1)], min_val=0, max_val=W * (-(-T // G) + 1))

        def next_first(eng, w):
            return eng.value_load(wtab[0:1, bass.ds(w * WCOLS + 4, 1)], min_val=0, max_val=T - 1)

        def first_tile(first, k):
            return nc.s_assert_within(first + k * G, 0, T - 1 + G, skip_runtime_bounds_check_because="a window's groups start at its tiles, which are below T, but for one group of padding")

        def flat(ap):
            return ap.rearrange("p o c -> p (o c)")

        def steps(names):
            return {n: i + 1 for i, n in enumerate(names)}

        def batch_steps(names):
            out, n = {}, 0
            for name in names:
                if name.endswith("*"):
                    for i in range(NB):
                        n += 1
                        out[name[:-1], i] = n
                else:
                    n += 1
                    out[name] = n
            return out, n

        NVS, NV = batch_steps(["load", "xm*", "st0*", "mv0*", "rs0", "h*", "xs*", "st1*", "mv1*", "rs1", "x1*", "dot*"])
        NAS, NA = batch_steps(["aggT*", "sqrt0", "hT*", "hid*", "sqrt1", "x1T*", "rows*"])
        NTS, NT = batch_steps(["aggT*", "y*", "hT*", "hid0", "hid1", "mlp0", "hid2", "mlp1", "hid3", "mlp2", "hid4", "mlp3", "mlp4",
                               "x1T*", "proj*"])
        NPS, NPL = batch_steps(["xbp", "xr", "xrb", "x1"])
        NDS = steps(["den0", "den1", "den2", "agg"])
        ND = len(NDS)
        GVS = steps(["agg", "y0", "y1", "st", "mv", "rs", "out"])
        GV = len(GVS)
        GAS = steps(["aggT", "sqrt"])
        GA = len(GAS)
        GTS = steps(["aggT", "y"])
        GT = len(GTS)
        FVS = steps(["d75", "den0", "den1", "den2", "feat"])
        feats = wide[:, :, 0:C]
        tbank = [pa, pn]
        spare = parts[:].rearrange("p w a c -> p (w a c)").bitcast(F32)
        node_max = spare[:, 0:NP]
        node_max_all = spare[:, NP:2 * NP]
        spare_b = parts[:].rearrange("p w a c -> p (w a c)")
        lo_hot = spare_b[:, 0:2 * DT * P].rearrange("p (b j n) -> p b j n", b=2, j=DT)
        hi_hot = spare_b[:, 2 * DT * P:2 * DT * (P + W)].rearrange("p (b j n) -> p b j n", b=2, j=DT)
        hi_ex = spare_b[:, 2 * DT * (P + W):2 * DT * (P + 4 * W)].rearrange("p (b j a n) -> p b j a n", b=2, j=DT, a=3)

        @block.sync
        def _(sp):
            for dst_ap, src_ap in GRAPH:
                sp.dma_start(dst_ap, src_ap).then_inc(s_graph, 16)
            for dst_ap, src_ap in CONSTS:
                sp.dma_start(dst_ap, src_ap).then_inc(s_const, 16)
            sp.sem_inc(xt_used, 1)
            with sp.Fori(0, W // NB) as it:
                sp.wait_ge(xt_used, it * NB + 1)
                sp.sem_inc(sp_seen, 1)
                for s in range(NB):
                    sp.dma_start(xt[:, s], io["xt"][bass.ds(it * NB + s, 1)].rearrange("o p k n -> p (o k) n")).then_inc(xt_in[s], 16)
            sp.wait_ge(wtab_done, 1)

            def group_tables(L, with_rows):
                def indices(tile, p):
                    sp.dma_start(idx[:, 2 * p:2 * p + 2], io["src"][:, bass.ds(tile + 2 * p, 2)]).then_inc(idx_in[L][p], 16)

                def load_rows(t0):
                    sp.dma_start(drow[:].rearrange("p j e -> p (j e)"),
                                 io["dst_r"][bass.ds(t0, G), :].rearrange("j e -> (j e)").partition_broadcast(P)).then_inc(drow_in[L], 16)

                def rows(v, t0):
                    sp.wait_ge(far[L], v + 2)
                    sp.sem_inc(sp_seen, 1)
                    load_rows(t0)

                def after_gathers(v, tile):
                    for p in range(PAIRS):
                        sp.wait_ge(gathered[L][2 * p], v * 16 + 16)
                        sp.sem_inc(sp_seen, 1)
                        sp.wait_ge(gathered[L][2 * p + 1], v * 16 + 16)
                        sp.sem_inc(sp_seen, 1)
                        indices(tile, p)

                start = sp.value_load(wtab[0:1, 0:1], min_val=0, max_val=T - 1)
                if L:
                    for p in range(PAIRS):
                        sp.wait_ge(idx_in[L - 1][p], total * 16 + 16)
                        sp.sem_inc(sp_seen, 1)
                    sp.wait_ge(drow_in[0], total * 16 + 16)
                    sp.sem_inc(sp_seen, 1)
                if with_rows:
                    load_rows(start)
                for p in range(PAIRS):
                    indices(start, p)
                with sp.Fori(0, W) as w:
                    first, groups, before = window(sp, w)
                    after = next_first(sp, w)
                    with sp.Fori(0, groups - 1) as k:
                        v = sp.snap(before + k)
                        if with_rows:
                            rows(v, first_tile(first, k + 1))
                        after_gathers(v, first_tile(first, k + 1))
                    v = last_group(sp, w)
                    if with_rows:
                        rows(v, after)
                    after_gathers(v, after)

            total = sp.snap(last_group(sp, W - 1) + 1)
            group_tables(0, True)
            with sp.Fori(0, W // NB) as it:
                sp.wait_ge(npl, it * NPL + 1)
                sp.sem_inc(sp_seen, 1)
                sp.dma_start(xw[:], io["x"][bass.ds(it * (NB * P), NB * P), :].rearrange("(w p) c -> p w c", p=P)).then_inc(xw_in, 16)
                for s in range(NB):
                    sp.wait_ge(nv, it * NV + NVS["dot", s] + 1)
                    sp.sem_inc(sp_seen, 1)
                    sp.wait_ge(na, it * NA + NAS["rows", s])
                    sp.sem_inc(sp_seen, 1)
                    sp.dma_start(proj_rows[bass.ds(it * (NB * P) + s * P, P), :], row[:, s]).then_inc(proj_stored, 16)
            group_tables(1, True)
            sp.wait_ge(fv, FVS["feat"])
            sp.dma_start(feat_rows.rearrange("(w p) c -> p w c", p=P), feats).then_inc(feat_stored, 16)
            group_tables(2, False)
            for p in range(PAIRS):
                sp.wait_ge(idx_in[2][p], total * 16 + 16)
                sp.sem_inc(sp_seen, 1)
            sp.wait_ge(drow_in[1], total * 16 + 16)
            sp.sem_inc(sp_seen, 1)

        @block.gpsimd
        def _(pool):
            pool.wait_ge(tables, 9)
            pool.partition_all_reduce(span_all[:].rearrange("p a w -> p (a w)"),
                                      span[:].rearrange("p a w -> p (a w)"), P,
                                      bass.bass_isa.ReduceOp.max).then_inc(span_red, 1)
            pool.wait_ge(wtab_done, 1)

            def gathers(L, rows, width):
                with pool.Fori(0, W) as w:
                    first, groups, before = window(pool, w)
                    with pool.Fori(0, groups) as k:
                        v = pool.snap(before + k)
                        for p in range(PAIRS):
                            pool.wait_ge(idx_in[L][p], v * 16 + 16)
                            pool.wait_ge(slots_free[L], v * PAIRS + p + 1)
                            pool.sem_inc(pool_seen, 1)
                            for j in (2 * p, 2 * p + 1):
                                pool.indirect_dma_start(
                                    out=gat[:, j, 0:width], out_offset=None, in_=rows,
                                    in_offset=bass.IndirectOffsetOnAxis(ap=idx[:, j:j + 1], axis=0)).then_inc(gathered[L][j], 16)

            for s in range(NB):
                pool.wait_ge(kv_stored[s], 16 * (W // NB) + 1)
            gathers(0, kv_rows, 2 * C)

            pool.sem_inc(npl, 1)
            with pool.Fori(0, W // NB) as it:
                pool.wait_ge(xw_in, it * 16 + 16)
                pool.wait_ge(nv, it * NV + 1)
                pool.tensor_tensor(xs[:], xw[:], bp[:].unsqueeze(1).broadcast_to([P, NB, C]), ALU.add).then_inc(npl, 1)
                pool.wait_ge(nv, it * NV + NVS["xm", NB - 1] + 1)
                pool.tensor_tensor(xw[:], xw[:], xm[:], ALU.add).then_inc(npl, 1)
                pool.wait_ge(npl, it * NPL + NPS["xr"] + 1)
                pool.tensor_tensor(xw[:], xw[:], b2[:].unsqueeze(1).broadcast_to([P, NB, C]), ALU.add).then_inc(npl, 1)
                pool.wait_ge(nv, it * NV + NVS["x1", NB - 1] + 1)
                pool.tensor_copy(x1[:, bass.ds(it * NB, NB), :], hn[:]).then_inc(npl, 1)

            pool.wait_ge(proj_stored, 16 * W + 1)
            gathers(1, proj_rows, CW)
            pool.wait_ge(ev, 2)
            pool.partition_all_reduce(rng_all[:], rng[:], P, bass.bass_isa.ReduceOp.max).then_inc(ep, 1)
            pool.wait_ge(slow_flag, 1)
            slow = pool.alloc_register("slow_pool")
            pool.reg_load(slow, slow_i[0:1, 0:1])
            with pool.If_ne(slow, 0):
                pool.wait_ge(slow_max, 1)
                pool.partition_all_reduce(node_max_all, node_max, P, bass.bass_isa.ReduceOp.max).then_inc(slow_all, 1)
            pool.wait_ge(feat_stored, 16)
            gathers(2, feat_rows, C)

        @block.tensor
        def _(pe):
            pe.wait_ge(s_const, CONST_ALL)
            with pe.Fori(0, W // NB) as it:
                for s in range(NB):
                    pe.wait_ge(xt_in[s], it * 16 + 16)
                    pe.wait_ge(qkv_out, it * (2 * NB) + (2 * (s - 2) if s >= 3 else 0) + 1)
                    b = 2 * (s % 3)
                    for k in range(KC):
                        pe.matmul(px[:, b, :], xt[:, s, k, :], wqkv[:, k, 0:2 * C], start=(k == 0), stop=(k == KC - 1))
                    for k in range(KC):
                        mm = pe.matmul(px[:, b + 1, 0:C], xt[:, s, k, :], wqkv[:, k, 2 * C:3 * C], start=(k == 0), stop=(k == KC - 1))
                    mm.then_inc(xt_used, 1)
            pe.wait_ge(wtab_done, 1)

            def expand(L, width, w, v, p):
                pe.wait_ge(hot_t[L], v * PAIRS + p + 2)
                if L == 0:
                    pe.wait_ge(mul1, v * PAIRS + p + 1)
                else:
                    pe.wait_ge(slots_free[1], v * PAIRS + p + 1)
                for j in (2 * p, 2 * p + 1):
                    for a in range(3):
                        mm = pe.matmul(px[:, j, 0:width], onehot_t[:, j, :], flat(parts[:, bass.ds(w, 1), a, 0:width]),
                                       start=(a == 0), stop=(a == 2))
                mm.then_inc(expd[L], 1)

            def open_window(L, width, w):
                pe.wait_ge(opened[L], w + 1)
                pe.matmul(pa[:, 0:width], zeros[:, 0:P], zeros[:, P:P + width], start=True, stop=True, skip_group_check=True)

            def sum_pair(v, p):
                pe.wait_ge(hot[0], v * PAIRS + p + 1)
                pe.wait_ge(msg1, v * PAIRS + p + 1)
                for j in (2 * p, 2 * p + 1):
                    mm = pe.matmul(pa[:, 0:C + H], onehot[:, j, :], msg[:, j, :], start=False, stop=True, skip_group_check=True)
                mm.then_inc(summed, 1)

            pe.wait_ge(q_ready, 1)
            with pe.Fori(0, W) as w:
                first, groups, before = window(pe, w)
                expand(0, C, w, before, 0)
                open_window(0, C + H, w)
                with pe.Fori(0, groups - 1) as k:
                    v = pe.snap(before + k)
                    expand(0, C, w, v, 1)
                    sum_pair(v, 0)
                    expand(0, C, w, v, 2)
                    sum_pair(v, 1)
                    expand(0, C, w, v + 1, 0)
                    sum_pair(v, 2)
                v = last_group(pe, w)
                expand(0, C, w, v, 1)
                sum_pair(v, 0)
                expand(0, C, w, v, 2)
                sum_pair(v, 1)
                sum_pair(v, 2)

            def transposed(bank, rows_s):
                for c in range(KC):
                    mm = pe.transpose(bank[:, c * P:(c + 1) * P], rows_s[:, c * P:(c + 1) * P], ident[:])
                mm.then_inc(nt, 1)


            with pe.Fori(0, W // NB) as it:
                def after_act(name, s=None):
                    pe.wait_ge(na, it * NA + NAS[name if s is None else (name, s)])

                def after_dve(name, s=None):
                    pe.wait_ge(nv, it * NV + NVS[name if s is None else (name, s)] + 1)

                after_dve("load")
                for s in range(NB):
                    if s >= 2:
                        after_act("aggT", s - 2)
                    transposed(tbank[s % 2], hn[:, s])
                for s in range(NB):
                    after_act("aggT", s)
                    if s >= 2:
                        after_dve("xm", s - 2)
                    for c in range(KC):
                        mm = pe.matmul(px[:, 4 + s % 2, 0:C], tr[:, s, c, :], wp[:, c, :], start=(c == 0), stop=(c == KC - 1))
                    mm.then_inc(nt, 1)
                for s in range(NB):
                    after_dve("h", s)
                    if s >= 2:
                        after_act("hT", s - 2)
                    transposed(tbank[s % 2], hn[:, s])

                def mlp_in(s):
                    after_act("hT", s)
                    if s >= 2:
                        after_act("hid", s - 2)
                    for f in range(NF):
                        for c in range(KC):
                            mm = pe.matmul(px[:, 2 * (s % 2) + f // 4, (f % 4) * P:(f % 4 + 1) * P], w1[:, c, f * P:(f + 1) * P],
                                           tr[:, s, c, :], start=(c == 0), stop=(c == KC - 1))
                    mm.then_inc(nt, 1)

                def mlp_out(s):
                    after_act("hid", s)
                    if s >= 2:
                        after_dve("xs", s - 2)
                    for f in range(NF):
                        mm = pe.matmul(px[:, 4 + s % 2, 0:C], hid[:, s % 2, f, :], w2[:, f, :], start=(f == 0), stop=(f == NF - 1))
                    mm.then_inc(nt, 1)

                mlp_in(0)
                for s in range(1, NB):
                    mlp_in(s)
                    mlp_out(s - 1)
                mlp_out(NB - 1)
                for s in range(NB):
                    after_dve("x1", s)
                    if s >= 2:
                        after_act("x1T", s - 2)
                    transposed(tbank[s % 2], hn[:, s])
                for s in range(NB):
                    after_act("x1T", s)
                    if s >= 4:
                        after_dve("dot", s - 4)
                    for c in range(KC):
                        mm = pe.matmul(px[:, s % 4, :], tr[:, s, c, :], wst[:, c, :], start=(c == 0), stop=(c == KC - 1))
                    mm.then_inc(nt, 1)

            pe.wait_ge(t_ready, 1)
            with pe.Fori(0, W) as w:
                first, groups, before = window(pe, w)
                with pe.Fori(0, groups) as k:
                    v = pe.snap(before + k)
                    for p in range(PAIRS):
                        expand(1, CW, w, v, p)

            pe.wait_ge(ea, 1)
            pe.matmul(pn[0:3 * W, 0:P], zeros[:, 0:3 * W], zeros[:, P:2 * P], start=True, stop=True, skip_group_check=True)
            with pe.Fori(0, T // DT // 2) as it:
                for b in range(2):
                    pe.wait_ge(dv, it * 10 + 5 * b + 5)
                    for j in range(DT):
                        mm = pe.matmul(pn[0:3 * W, 0:P], hi_ex[:, b, j].rearrange("p a n -> p (a n)"), lo_hot[:, b, j, :],
                                       start=False, stop=True, skip_group_check=True)
                    mm.then_inc(dpe, 1)
            pe.wait_ge(fv, FVS["d75"])
            pe.matmul(pn[:, P:P + W], d75[:], pick[:], start=True, stop=True).then_inc(fpe, 1)

            with pe.Fori(0, W) as w:
                first, groups, before = window(pe, w)
                open_window(1, C, w)
                with pe.Fori(0, groups) as k:
                    v = pe.snap(before + k)
                    for p in range(PAIRS):
                        pe.wait_ge(hot[1], v * PAIRS + p + 1)
                        for j in (2 * p, 2 * p + 1):
                            pe.wait_ge(gathered[2][j], v * 16 + 16)
                            mm = pe.matmul(pa[:, 0:C], onehot[:, j, :], gat[:, j, 0:C], start=False, stop=True, skip_group_check=True)
                        mm.then_inc(slots_free[2], 1)
                pe.wait_ge(gv, w * GV + GVS["agg"])
                for c in range(KC):
                    mm = pe.transpose(pn[:, c * P:(c + 1) * P], agg[:, c * P:(c + 1) * P], ident[:])
                mm.then_inc(gt, 1)
                pe.wait_ge(ga, w * GA + GAS["aggT"])
                for c in range(KC):
                    mm = pe.matmul(pn[:, C:2 * C], tr[:, 0, c, :], wfc[:, c, :], start=(c == 0), stop=(c == KC - 1))
                mm.then_inc(gt, 1)

        @block.scalar
        def _(act):
            for s in range(NB):
                act.sem_inc(kv_stored[s], 1)
            with act.Fori(0, W // NB) as it:
                for s in range(NB):
                    act.wait_ge(kv_row_ready, it * NB + s + 1)
                    act.dma_start(kv_rows[bass.ds(it * (NB * P) + s * P, P), :], gat[:, s, :]).then_inc(kv_stored[s], 16)
            act.wait_ge(wtab_done, 1)
            for L in (0, 1):
                act.sem_inc(far[L], 1)
                act.sem_inc(hot_t[L], 1)

            def node_distances(L, w, v):
                act.wait_ge(drow_in[L], v * 16 + 16)
                act.wait_ge(hot_t[L], v * PAIRS + 1)
                act.sem_inc(act_seen, 1)
                act.activation(away_t[:], drow[:], ACT.Abs, bias=nnode[:, bass.ds(w, 1)]).then_inc(far[L], 1)

            def node_onehots(L, v, p):
                if p == 0:
                    act.wait_ge(far[L], v + 2)
                act.wait_ge(expd[L], v * PAIRS + p + 1)
                act.activation(onehot_t[:, 2 * p:2 * p + 2, :], away_t[:, 2 * p:2 * p + 2, :], ACT.Relu, bias=1.0, scale=-1.0).then_inc(hot_t[L], 1)

            def edge_distances(v, t0, p):
                for j in (2 * p, 2 * p + 1):
                    ins = act.activation(away[:, j, :], iota_w[:], ACT.Abs, bias=ndst_f[:, bass.ds(t0 + j, 1)])
                ins.then_inc(far_e, 1)

            def edge_onehots(v, p):
                act.wait_ge(far_e, v * PAIRS + p + 1)
                act.wait_ge(summed, v * PAIRS + p + 1)
                act.activation(onehot[:, 2 * p:2 * p + 2, :], away[:, 2 * p:2 * p + 2, :], ACT.Relu, bias=1.0, scale=-1.0).then_inc(hot[0], 1)

            def exps(v, p):
                act.wait_ge(clp1, v * PAIRS + p + 1)
                act.wait_ge(summed, v * PAIRS + p + 1)
                act.activation(msg[:, 2 * p:2 * p + 2, C:C + H], score[:, p], ACT.Exp, scale=SCORE_SCALE).then_inc(exp1, 1)

            with act.Fori(0, W) as w:
                first, groups, before = window(act, w)
                act.wait_ge(hot[0], before * PAIRS + 1)
                act.sem_inc(act_seen, 1)
                act.activation(iota_w[:], iota[:], ACT.Identity, bias=wlo[:, bass.ds(w, 1)]).then_inc(iotaw_set, 1)
                act.wait_ge(iotaw_set, w + 1)
                t0 = first_tile(first, 0)
                node_distances(0, w, before)
                for p in range(PAIRS):
                    node_onehots(0, before, p)
                    edge_distances(before, t0, p)
                edge_onehots(before, 0)
                edge_onehots(before, 1)
                with act.Fori(0, groups - 1) as k:
                    v = act.snap(before + k)
                    t1 = first_tile(first, k + 1)
                    exps(v, 0)
                    node_distances(0, w, v + 1)
                    node_onehots(0, v + 1, 0)
                    edge_distances(v + 1, t1, 0)
                    edge_onehots(v, 2)
                    exps(v, 1)
                    node_onehots(0, v + 1, 1)
                    edge_distances(v + 1, t1, 1)
                    edge_onehots(v + 1, 0)
                    exps(v, 2)
                    node_onehots(0, v + 1, 2)
                    edge_distances(v + 1, t1, 2)
                    edge_onehots(v + 1, 1)
                v = last_group(act, w)
                exps(v, 0)
                edge_onehots(v, 2)
                exps(v, 1)
                exps(v, 2)

            with act.Fori(0, W // NB) as it:
                def after_pe(name, s=None):
                    act.wait_ge(nt, it * NT + NTS[name if s is None else (name, s)])

                def after_dve(name, s=None):
                    act.wait_ge(nv, it * NV + NVS[name if s is None else (name, s)] + 1)

                for s in range(NB):
                    after_pe("aggT", s)
                    act.copy(tr[:, s], tbank[s % 2][:, 0:C].rearrange("p (k n) -> p k n", k=KC)).then_inc(na, 1)
                after_dve("mv0", NB - 1)
                act.activation(rstd[:, 0, :], mv[:, :, 1], ACT.Sqrt, bias=eps[:, 0:1]).then_inc(na, 1)
                for s in range(NB):
                    after_pe("hT", s)
                    for c in range(KC):
                        ins = act.activation(tr[:, s, c, :], tbank[s % 2][:, c * P:(c + 1) * P], ACT.Identity, bias=lnb[:, c:c + 1], scale=lng[:, c:c + 1])
                    ins.then_inc(na, 1)
                for s in range(NB):
                    after_pe(f"hid{s}")
                    if s >= 2:
                        after_pe(f"mlp{s - 2}")
                    for f in range(NF):
                        ins = act.activation(hid[:, s % 2, f, :], px[:, 2 * (s % 2) + f // 4, (f % 4) * P:(f % 4 + 1) * P], ACT.Gelu, bias=b1[:, f:f + 1])
                    ins.then_inc(na, 1)
                after_dve("mv1", NB - 1)
                act.activation(rstd[:, 0, :], mv[:, :, 1], ACT.Sqrt, bias=eps[:, 0:1]).then_inc(na, 1)
                for s in range(NB):
                    after_pe("x1T", s)
                    act.copy(tr[:, s], tbank[s % 2][:, 0:C].rearrange("p (k n) -> p k n", k=KC)).then_inc(na, 1)
                for s in range(NB):
                    after_pe("proj", s)
                    act.wait_ge(proj_stored, it * (16 * NB) + 1)
                    act.copy(row[:, s, 0:C], px[:, s % 4, 0:C])
                    act.copy(flat(wide[:, bass.ds(it * NB + s, 1), 0:C]), px[:, s % 4, C:2 * C]).then_inc(na, 1)

            with act.Fori(0, W) as w:
                first, groups, before = window(act, w)
                with act.Fori(0, groups) as k:
                    v = act.snap(before + k)
                    node_distances(1, w, v)
                    for p in range(PAIRS):
                        node_onehots(1, v, p)
            act.wait_ge(ev, 6)
            act.activation(e_all[:], e_all[:], ACT.Exp, bias=shift[:, 0:1]).then_inc(ea, 1)
            act.sem_inc(out_stored, 1)
            with act.Fori(0, W - 1) as w:
                act.wait_ge(gt, w * GT + GTS["aggT"])
                act.copy(tr[:, 0], pn[:, 0:C].rearrange("p (k n) -> p k n", k=KC)).then_inc(ga, 1)
                act.wait_ge(gv, w * GV + GVS["mv"])
                act.activation(rstd[:, 0, 0:1], mv[:, 0, 1:2], ACT.Sqrt, bias=eps[:, 0:1]).then_inc(ga, 1)
                act.wait_ge(gv, w * GV + GV)
                act.dma_start(io["out"][bass.ds(w * P, P), :], hn[:, 0]).then_inc(out_stored, 16)
            act.wait_ge(gt, (W - 1) * GT + GTS["aggT"])
            act.copy(tr[:, 0], pn[:, 0:C].rearrange("p (k n) -> p k n", k=KC)).then_inc(ga, 1)
            act.wait_ge(gv, (W - 1) * GV + GVS["mv"])
            act.activation(rstd[:, 0, 0:1], mv[:, 0, 1:2], ACT.Sqrt, bias=eps[:, 0:1]).then_inc(ga, 1)
            act.wait_ge(gv, W * GV)
            act.dma_start(io["out"][(W - 1) * P:N_NODES, :], hn[0:N_NODES - (W - 1) * P, 0]).then_inc(out_stored, 16)
            act.wait_ge(out_stored, 16 * W + 1)

        @block.vector
        def _(dve):
            dve.memset(eps[:], EPS).then_inc(tables, 1)
            dve.memset(zeros[:], 0.0).then_inc(tables, 1)
            dve.wait_ge(s_graph, GRAPH_ALL)
            dve.wait_ge(s_const, CONST_ALL)
            dve.tensor_reduce(tile_lo[:], dst_rows, AX, ALU.min).then_inc(tables, 1)
            dve.tensor_reduce(tile_hi[:], dst_rows, AX, ALU.max).then_inc(tables, 1)
            dve.wait_ge(tables, 4)
            lo_b = tile_lo[:].unsqueeze(1).broadcast_to([P, W, TB])
            hi_b = tile_hi[:].unsqueeze(1).broadcast_to([P, W, TB])
            dve.tensor_tensor(hit2[:, 0], lo_b, tcon[:, 1], ALU.is_le).then_inc(tables, 1)
            dve.tensor_tensor(hit2[:, 1], hi_b, tcon[:, 0], ALU.is_ge).then_inc(tables, 1)
            dve.wait_ge(tables, 6)
            dve.tensor_tensor(hit[:], hit2[:, 0], hit2[:, 1], ALU.mult).then_inc(tables, 1)
            dve.wait_ge(tables, 7)
            dve.tensor_tensor(hit2[:], hit[:].unsqueeze(1).broadcast_to([P, 2, W, TB]), tcon[:, 2:4], ALU.mult).then_inc(tables, 1)
            dve.wait_ge(tables, 8)
            dve.tensor_reduce(span[:], hit2[:], AX, ALU.max).then_inc(tables, 1)
            dve.tensor_scalar(ndst_f[:], dst_i[:], -1.0, None, ALU.mult).then_inc(tables, 1)
            dve.tensor_copy(src_f[:], src_i[:]).then_inc(tables, 1)
            dve.wait_ge(tables, 10)
            dve.tensor_scalar(dst_i[:], src_i[:], 7, None, ALU.arith_shift_right).then_inc(tables, 1)
            dve.wait_ge(tables, 12)
            dve.tensor_copy(src_hi[:], dst_i[:]).then_inc(tables, 1)
            dve.wait_ge(tables, 13)
            dve.scalar_tensor_tensor(out=src_lob[:], in0=src_hi[:], scalar=float(-P), in1=src_f[:], op0=ALU.mult, op1=ALU.add).then_inc(tables, 1)
            dve.tensor_scalar(attn_lo[:], attn[:], SLOPE, None, ALU.mult).then_inc(tables, 1)
            dve.tensor_scalar(attn_hi[:], attn[:], 1.0 - SLOPE, None, ALU.mult).then_inc(tables, 1)
            dve.memset(e_all[:], 0.0).then_inc(tables, 1)
            dve.memset(wide[:, :, C + 1:C + 2], 1.0).then_inc(tables, 1)
            dve.tensor_copy(src_hib[:], src_hi[:]).then_inc(tables, 1)
            dve.tensor_copy(iota_b[:], iota[:]).then_inc(tables, 1)
            n = 20
            dve.wait_ge(span_red, 1)
            end, start = span_all[0:1, 0, :], span_all[0:1, 1, :]

            def link(ins):
                nonlocal n
                n += 1
                ins.then_inc(tables, 1)
                dve.wait_ge(tables, n)

            link(dve.tensor_scalar(wf[:, 0], start, -1.0, float(TPAD), ALU.mult, ALU.add))
            link(dve.tensor_scalar(wf[:, 0], wf[:, 0], float(T - 1), None, ALU.min))
            link(dve.tensor_tensor(wf[:, 1], end, wf[:, 0], ALU.subtract))
            link(dve.tensor_scalar(wf[:, 1], wf[:, 1], float(G - 1), float(2 * G), ALU.add, ALU.max))
            link(dve.tensor_scalar(wf[:, 1], wf[:, 1], 1.0 / G, -0.5 + 0.5 / G, ALU.mult, ALU.add))
            link(dve.tensor_scalar(wf[:, 1], wf[:, 1], 8388608.0, None, ALU.add))
            link(dve.tensor_scalar(wf[:, 1], wf[:, 1], -8388608.0, None, ALU.add))
            link(dve.memset(wf[:, 3], 0.0))
            link(dve.tensor_tensor_scan(wf[:, 2], wf[:, 1], wf[:, 3], 0.0, ALU.add, ALU.add))
            link(dve.tensor_scalar(wf[:, 3], wf[:, 2], -1.0, None, ALU.add))
            link(dve.tensor_tensor(wf[:, 2], wf[:, 2], wf[:, 1], ALU.subtract))
            link(dve.tensor_copy(wf[:, 4, 0:W - 1], wf[:, 0, 1:W]))
            link(dve.tensor_copy(wf[:, 4, W - 1:W], wf[:, 0, W - 1:W]))
            link(dve.tensor_copy(wtab[:].rearrange("o (w a) -> o a w", a=WCOLS), wf[:]))
            dve.sem_inc(wtab_done, 1)

            dve.sem_inc(qkv_out, 1)
            with dve.Fori(0, W // NB) as it:
                for s in range(NB):
                    b = 2 * (s % 3)
                    dve.wait_ge(xt_used, it * NB + s + 2)
                    dve.wait_ge(kv_stored[s], it * 16 + 1)
                    dve.tensor_tensor(gat[:, s, :], px[:, b, :], bqkv[:, 0:2 * C], ALU.add).then_inc(kv_row_ready, 1)
                    dve.wait_ge(kv_row_ready, it * NB + s + 1)
                    dve.sem_inc(qkv_out, 1)
                    dve.tensor_tensor(wide[:, bass.ds(it * NB + s, 1), 0:C].rearrange("p o c -> p (o c)"), px[:, b + 1, 0:C], bqkv[:, 2 * C:3 * C], ALU.add).then_inc(qkv_out, 1)

            def split(width, base):
                m = base
                for a in range(3):
                    dve.tensor_copy(parts[:, :, a, 0:width], wide[:, :, 0:width]).then_inc(split_v, 1)
                    m += 1
                    dve.wait_ge(split_v, m)
                    if a < 2:
                        dve.tensor_tensor(wide[:, :, 0:width], wide[:, :, 0:width], parts[:, :, a, 0:width], ALU.subtract).then_inc(split_v, 1)
                        m += 1
                        dve.wait_ge(split_v, m)
                return m

            dve.wait_ge(qkv_out, 2 * W + 1)
            m = split(C, 0)
            dve.sem_inc(q_ready, 1)

            dve.sem_inc(summed, PAIRS)
            dve.sem_inc(opened[0], 1)
            dve.sem_inc(mul1, PAIRS)
            dve.sem_inc(slots_free[0], PAIRS)
            dve.sem_inc(slots_free[1], PAIRS)
            dve.sem_inc(expd[0], PAIRS)
            dve.sem_inc(expd[1], PAIRS)
            dve.sem_inc(hot[0], 1)
            dve.sem_inc(proj_stored, 1)

            def products(v, p):
                dve.wait_ge(expd[0], v * PAIRS + p + 1 + PAIRS)
                for j in (2 * p, 2 * p + 1):
                    dve.wait_ge(gathered[0][j], v * 16 + 16)
                dve.tensor_tensor(prod[:, p % 2].rearrange("p (j c) -> p j c", j=2), px[:, 2 * p:2 * p + 2, 0:C],
                                  gat[:, 2 * p:2 * p + 2, 0:C], ALU.mult).then_inc(mul1, 1)

            def scores(v, p):
                dve.wait_ge(mul1, v * PAIRS + p + 1 + PAIRS)
                if p < 0:
                    pass
                dve.tensor_reduce(score[:, p], prod[:, p % 2].rearrange("p (j h d) -> p j h d", j=2, h=H), AX, ALU.add).then_inc(red1, 1)
                dve.wait_ge(red1, v * PAIRS + p + 1)
                dve.tensor_scalar(score[:, p], score[:, p], CLIP, -CLIP, ALU.min, ALU.max).then_inc(clp1, 1)

            def messages(v, p):
                dve.wait_ge(exp1, v * PAIRS + p + 1)
                dve.tensor_tensor(msg[:, 2 * p:2 * p + 2, 0:C].rearrange("p j (h d) -> p j h d", h=H),
                                  gat[:, 2 * p:2 * p + 2, C:2 * C].rearrange("p j (h d) -> p j h d", h=H),
                                  msg[:, 2 * p:2 * p + 2, C:C + H].unsqueeze(3).broadcast_to([P, 2, H, HD]),
                                  ALU.mult).then_inc(msg1, 1)

            def freed(v, p):
                dve.wait_ge(msg1, v * PAIRS + p + 1)
                dve.sem_inc(slots_free[0], 1)

            with dve.Fori(0, W) as w:
                first, groups, before = window(dve, w)
                products(before, 0)
                scores(before, 0)
                with dve.Fori(0, groups - 1) as k:
                    v = dve.snap(before + k)
                    for p in range(PAIRS):
                        n_v, n_p = (v, p + 1) if p + 1 < PAIRS else (v + 1, 0)
                        products(n_v, n_p)
                        messages(v, p)
                        scores(n_v, n_p)
                        freed(v, p)
                v = last_group(dve, w)
                for p in range(PAIRS):
                    if p + 1 < PAIRS:
                        products(v, p + 1)
                    messages(v, p)
                    if p + 1 < PAIRS:
                        scores(v, p + 1)
                    freed(v, p)
                dve.wait_ge(summed, (before + groups) * PAIRS + PAIRS)
                dve.tensor_scalar(den[:, 0], pa[:, C:C + H], 0.0, None, ALU.is_equal).then_inc(nd, 1)
                dve.wait_ge(nd, w * ND + NDS["den0"])
                dve.tensor_tensor(den[:, 1], den[:, 0], pa[:, C:C + H], ALU.add).then_inc(nd, 1)
                dve.wait_ge(nd, w * ND + NDS["den1"])
                dve.reciprocal(den[:, 2], den[:, 1]).then_inc(nd, 1)
                dve.wait_ge(nd, w * ND + NDS["den2"])
                dve.tensor_tensor(flat(wide[:, bass.ds(w, 1), 0:C]).rearrange("p (h d) -> p h d", h=H), pa[:, 0:C].rearrange("p (h d) -> p h d", h=H),
                                  den[:, 2].unsqueeze(2).broadcast_to([P, H, HD]), ALU.mult).then_inc(nd, 1)
                dve.wait_ge(nd, w * ND + NDS["agg"])
                dve.sem_inc(opened[0], 1)

            dve.sem_inc(nv, 1)
            dve.memset(row[:, :, C + 1:C + 2], 0.0).then_inc(split_v, 1)
            m += 1
            with dve.Fori(0, W // NB) as it:
                def at(name, s=None):
                    return it * NV + NVS[name if s is None else (name, s)] + 1

                def after_pe(name, s=None):
                    dve.wait_ge(nt, it * NT + NTS[name if s is None else (name, s)])

                dve.wait_ge(npl, it * NPL + 1)
                dve.tensor_copy(hn[:], wide[:, bass.ds(it * NB, NB), 0:C]).then_inc(nv, 1)
                dve.wait_ge(npl, it * NPL + NPS["xbp"] + 1)
                for s in range(NB):
                    after_pe("y", s)
                    dve.tensor_tensor(xm[:, s], px[:, 4 + s % 2, 0:C], xs[:, s], ALU.add).then_inc(nv, 1)
                for s in range(NB):
                    dve.wait_ge(nv, at("xm", s))
                    dve.bn_stats(stats[:, s], xm[:, s]).then_inc(nv, 1)
                for s in range(NB):
                    dve.wait_ge(nv, at("st0", s))
                    dve.sem_inc(dve_seen, 1)
                    dve.bn_aggr(mv[:, s], stats[:, s]).then_inc(nv, 1)
                dve.wait_ge(na, it * NA + NAS["sqrt0"])
                dve.reciprocal(rstd[:, 1, :], rstd[:, 0, :]).then_inc(nv, 1)
                dve.wait_ge(nv, at("rs0"))
                for s in range(NB):
                    dve.tensor_scalar(hn[:, s], xm[:, s], mv[:, s, 0:1], rstd[:, 1, s:s + 1], ALU.subtract, ALU.mult).then_inc(nv, 1)
                dve.wait_ge(npl, it * NPL + NPS["xrb"] + 1)
                for s in range(NB):
                    after_pe(f"mlp{s}")
                    dve.tensor_tensor(xs[:, s], px[:, 4 + s % 2, 0:C], xw[:, s], ALU.add).then_inc(nv, 1)
                for s in range(NB):
                    dve.wait_ge(nv, at("xs", s))
                    dve.bn_stats(stats[:, s], xs[:, s]).then_inc(nv, 1)
                for s in range(NB):
                    dve.wait_ge(nv, at("st1", s))
                    dve.sem_inc(dve_seen, 1)
                    dve.bn_aggr(mv[:, s], stats[:, s]).then_inc(nv, 1)
                dve.wait_ge(na, it * NA + NAS["sqrt1"])
                dve.reciprocal(rstd[:, 1, :], rstd[:, 0, :]).then_inc(nv, 1)
                dve.wait_ge(nv, at("rs1"))
                for s in range(NB):
                    dve.tensor_scalar(hn[:, s], xs[:, s], mv[:, s, 0:1], rstd[:, 1, s:s + 1], ALU.subtract, ALU.mult).then_inc(nv, 1)
                for s in range(NB):
                    dve.wait_ge(na, it * NA + NAS["rows", s])
                    dve.scalar_tensor_tensor(out=prod[:, 0, 0:C], in0=px[:, s % 4, 0:C], scalar=1.0, in1=attn_lo[:], op0=ALU.mult, op1=ALU.mult,
                                             accum_out=row[:, s, C:C + 1])
                    dve.scalar_tensor_tensor(out=prod[:, 1, 0:C], in0=px[:, s % 4, C:2 * C], scalar=1.0, in1=attn_lo[:], op0=ALU.mult, op1=ALU.mult,
                                             accum_out=flat(wide[:, bass.ds(it * NB + s, 1), C:C + 1])).then_inc(nv, 1)
                    dve.wait_ge(nv, at("dot", s))

            dve.wait_ge(na, (W // NB) * NA)
            m = split(CW, m)
            dve.sem_inc(t_ready, 1)
            ZSTEPS = PAIRS + G + 4
            with dve.Fori(0, W) as w:
                first, groups, before = window(dve, w)
                with dve.Fori(0, groups) as k:
                    v = dve.snap(before + k)
                    t0 = first_tile(first, k)

                    def rows(p):
                        dve.wait_ge(expd[1], v * PAIRS + p + 1 + PAIRS)
                        for j in (2 * p, 2 * p + 1):
                            dve.wait_ge(gathered[1][j], v * 16 + 16)
                        dve.tensor_tensor(zbuf[:, 2 * p:2 * p + 2, :], px[:, 2 * p:2 * p + 2, 0:CW], gat[:, 2 * p:2 * p + 2, 0:CW], ALU.add).then_inc(zs, 1)

                    def attend(p, count):
                        dve.wait_ge(zs, v * ZSTEPS + count)
                        dve.sem_inc(slots_free[1], 1)
                        for j in (2 * p, 2 * p + 1):
                            dve.scalar_tensor_tensor(out=prod[:, j % 2, 0:C] if p % 2 else prod[:, j % 2, C:2 * C], in0=zbuf[:, j, 0:C], scalar=0.0, in1=attn_hi[:],
                                                     op0=ALU.max, op1=ALU.mult, accum_out=dots[:, 0, j:j + 1]).then_inc(zs, 1)

                    rows(0)
                    rows(1)
                    attend(0, 1)
                    rows(2)
                    attend(1, 2)
                    attend(2, 5)
                    dve.wait_ge(zs, v * ZSTEPS + PAIRS + G)
                    dve.tensor_tensor(dots[:, 1], dots[:, 0], zbuf[:, :, C], ALU.add).then_inc(zs, 1)
                    dve.wait_ge(zs, v * ZSTEPS + PAIRS + G + 1)
                    dve.tensor_tensor(dots[:, 2], dots[:, 1], zbuf[:, :, C + 1], ALU.mult).then_inc(zs, 1)
                    dve.wait_ge(zs, v * ZSTEPS + PAIRS + G + 2)
                    dve.tensor_tensor(e_all[:, bass.ds(t0, G)], e_all[:, bass.ds(t0, G)], dots[:, 2], ALU.add).then_inc(zs, 1)
                    dve.wait_ge(zs, v * ZSTEPS + PAIRS + G + 3)
                    dve.sem_inc(zs, 1)

            dve.memset(e_all[:, T:TPAD], -FAR).then_inc(sv, 1)
            dve.tensor_reduce(rng[:, 0:1], e_all[:, 0:T], AX, ALU.max).then_inc(ev, 1)
            dve.tensor_reduce(dots[:, 0, 0:1], e_all[:, 0:T], AX, ALU.min).then_inc(sv, 1)
            dve.wait_ge(sv, 2)
            dve.tensor_scalar(rng[:, 1:2], dots[:, 0, 0:1], -1.0, None, ALU.mult).then_inc(ev, 1)
            dve.wait_ge(ep, 1)
            dve.tensor_tensor(dots[:, 1, 0:1], rng_all[:, 0:1], rng_all[:, 1:2], ALU.add).then_inc(ev, 1)
            dve.wait_ge(ev, 3)
            dve.tensor_scalar(slow_i[:], dots[0:1, 1, 0:1], SPREAD, None, ALU.is_gt).then_inc(ev, 1)
            dve.tensor_scalar(shift[:], rng_all[:, 0:1], -1.0, None, ALU.mult).then_inc(ev, 1)
            dve.wait_ge(ev, 5)
            dve.sem_inc(slow_flag, 1)
            slow = dve.alloc_register("slow_dve")
            dve.reg_load(slow, slow_i[0:1, 0:1])
            count, pen, masked, m_edge = dots[:, 2, 0:1], gat[:, 0:2].rearrange("p j c -> p (j c)")[:, 0:T], \
                gat[:, 2:4].rearrange("p j c -> p (j c)")[:, 0:T], gat[:, 4:6].rearrange("p j c -> p (j c)")[:, 0:T]
            with dve.If_ne(slow, 0):
                dve.memset(count, 0.0).then_inc(sv, 1)
                dve.memset(m_edge, 0.0).then_inc(sv, 1)
                with dve.Fori(0, NP) as node:
                    dve.wait_ge(sv, node * 4 + 4)
                    dve.tensor_scalar(pen, src_f[:, 0:T], count, -FAR, ALU.not_equal, ALU.mult).then_inc(sv, 1)
                    dve.wait_ge(sv, node * 4 + 5)
                    dve.tensor_tensor(masked, e_all[:, 0:T], pen, ALU.add).then_inc(sv, 1)
                    dve.wait_ge(sv, node * 4 + 6)
                    dve.tensor_reduce(node_max[:, bass.ds(node, 1)], masked, AX, ALU.max).then_inc(sv, 1)
                    dve.wait_ge(sv, node * 4 + 7)
                    dve.tensor_scalar(count, count, 1.0, None, ALU.add).then_inc(sv, 1)
                dve.wait_ge(sv, NP * 4 + 4)
                dve.sem_inc(slow_max, 1)
                dve.wait_ge(slow_all, 1)
                dve.memset(count, 0.0).then_inc(sv, 1)
                with dve.Fori(0, NP) as node:
                    dve.wait_ge(sv, node * 3 + NP * 4 + 5)
                    dve.tensor_scalar(pen, src_f[:, 0:T], count, node_max_all[:, bass.ds(node, 1)], ALU.is_equal, ALU.mult).then_inc(sv, 1)
                    dve.wait_ge(sv, node * 3 + NP * 4 + 6)
                    dve.tensor_tensor(m_edge, m_edge, pen, ALU.add).then_inc(sv, 1)
                    dve.wait_ge(sv, node * 3 + NP * 4 + 7)
                    dve.tensor_scalar(count, count, 1.0, None, ALU.add).then_inc(sv, 1)
                dve.wait_ge(sv, NP * 7 + 5)
                dve.tensor_tensor(e_all[:, 0:T], e_all[:, 0:T], m_edge, ALU.subtract).then_inc(sv, 1)
                dve.memset(shift[:], 0.0).then_inc(sv, 1)
                dve.wait_ge(sv, NP * 7 + 7)
            dve.sem_inc(ev, 1)

            dve.wait_ge(ea, 1)
            rest = gat[:, 0:2].rearrange("p j c -> p (j c)")[:, 0:T]
            from_e = e_all[:, 0:T]
            for a in range(3):
                dve.tensor_copy(e_parts[:, a], from_e).then_inc(dsplit, 1)
                dve.wait_ge(dsplit, 2 * a + 1)
                if a < 2:
                    dve.tensor_tensor(rest, from_e, e_parts[:, a], ALU.subtract).then_inc(dsplit, 1)
                    dve.wait_ge(dsplit, 2 * a + 2)
                    from_e = rest
            dve.sem_inc(dpe, 2)
            with dve.Fori(0, T // DT // 2) as it:
                for b in range(2):
                    dve.wait_ge(dpe, it * 2 + b + 1)
                    t0 = it * (2 * DT) + b * DT
                    dve.tensor_tensor(hi_hot[:, b], iota_b[:, 0:W].unsqueeze(1).broadcast_to([P, DT, W]),
                                      src_hib[:, bass.ds(t0, DT)].unsqueeze(2).broadcast_to([P, DT, W]), ALU.is_equal).then_inc(dv, 1)
                    dve.tensor_tensor(lo_hot[:, b], iota_b[:].unsqueeze(1).broadcast_to([P, DT, P]),
                                      src_lob[:, bass.ds(t0, DT)].unsqueeze(2).broadcast_to([P, DT, P]), ALU.is_equal).then_inc(dv, 1)
                    dve.wait_ge(dv, it * 10 + 5 * b + 1)
                    for a in range(3):
                        dve.tensor_tensor(hi_ex[:, b, :, a, :], hi_hot[:, b],
                                          e_parts[:, a, bass.ds(t0, DT)].unsqueeze(2).broadcast_to([P, DT, W]), ALU.mult).then_inc(dv, 1)
            dve.wait_ge(dpe, T // DT + 2)
            dve.tensor_copy(d75[:], pn[0:3 * W, 0:P]).then_inc(fv, 1)
            dve.wait_ge(fpe, 1)
            dve.tensor_scalar(denom[:, 0], pn[:, P:P + W], 0.0, None, ALU.is_equal).then_inc(fv, 1)
            dve.wait_ge(fv, 2)
            dve.tensor_tensor(denom[:, 1], denom[:, 0], pn[:, P:P + W], ALU.add).then_inc(fv, 1)
            dve.wait_ge(fv, 3)
            dve.reciprocal(denom[:, 2], denom[:, 1]).then_inc(fv, 1)
            dve.wait_ge(fv, 4)
            dve.tensor_tensor(feats, x1[:], denom[:, 2].unsqueeze(2).broadcast_to([P, W, C]), ALU.mult).then_inc(fv, 1)

            dve.sem_inc(opened[1], 1)
            dve.sem_inc(slots_free[2], PAIRS)
            with dve.Fori(0, W) as w:
                first, groups, before = window(dve, w)
                with dve.Fori(0, groups) as k:
                    v = dve.snap(before + k)
                    t0 = first_tile(first, k)
                    dve.tensor_scalar(dst_g[:], ndst_f[:, bass.ds(t0, G)], -1.0, wlo[:, bass.ds(w, 1)], ALU.mult, ALU.subtract).then_inc(dgs, 1)
                    dve.tensor_copy(ex_g[:], e_all[:, bass.ds(t0, G)]).then_inc(dgs, 1)
                    dve.wait_ge(dgs, v * 2 + 2)
                    for p in range(PAIRS):
                        dve.wait_ge(slots_free[2], v * PAIRS + p + 1)
                        for j in (2 * p, 2 * p + 1):
                            ins = dve.tensor_scalar(onehot[:, j, :], iota[:], dst_g[:, j:j + 1], ex_g[:, j:j + 1], ALU.is_equal, ALU.mult)
                        ins.then_inc(hot[1], 1)
                    dve.wait_ge(hot[1], v * PAIRS + PAIRS)
                dve.wait_ge(slots_free[2], (before + groups) * PAIRS + PAIRS)

                def at(name):
                    return w * GV + GVS[name]

                dve.tensor_copy(agg[:], pa[:, 0:C]).then_inc(gv, 1)
                dve.wait_ge(gv, at("agg"))
                dve.sem_inc(opened[1], 1)
                dve.wait_ge(gt, w * GT + GTS["y"])
                dve.tensor_tensor(xm[:, 0], pn[:, C:2 * C], bfc[:], ALU.add).then_inc(gv, 1)
                dve.wait_ge(gv, at("y0"))
                dve.tensor_tensor(xm[:, 0], xm[:, 0], flat(x1[:, bass.ds(w, 1), :]), ALU.add).then_inc(gv, 1)
                dve.wait_ge(gv, at("y1"))
                dve.bn_stats(stats[:, 0], xm[:, 0]).then_inc(gv, 1)
                dve.wait_ge(gv, at("st"))
                dve.sem_inc(dve_seen, 1)
                dve.bn_aggr(mv[:, 0], stats[:, 0]).then_inc(gv, 1)
                dve.wait_ge(ga, w * GA + GAS["sqrt"])
                dve.reciprocal(rstd[:, 1, 0:1], rstd[:, 0, 0:1]).then_inc(gv, 1)
                dve.wait_ge(gv, at("rs"))
                dve.wait_ge(out_stored, w * 16 + 1)
                dve.tensor_scalar(hn[:, 0], xm[:, 0], mv[:, 0, 0:1], rstd[:, 1, 0:1], ALU.subtract, ALU.mult).then_inc(gv, 1)


INPUTS = ["src", "dst", "dst_r", "x", "xt", "wqkv", "bqkv", "wp", "bp", "lng", "lnb", "w1", "b1", "w2", "b2",
          "wst", "attn", "wfc", "bfc", "c_iota", "c_ident", "c_wlo", "c_nnode", "c_pick", "c_tcon"]


def shape_constants():
    window = np.arange(W, dtype=np.float32) * P
    tile = (np.arange(TB)[None, :] * P + np.arange(P)[:, None]).astype(np.float32)
    grid = np.empty((P, 4, W, TB), np.float32)
    grid[:, 0] = window[None, :, None]
    grid[:, 1] = window[None, :, None] + (P - 1)
    grid[:, 2] = tile[:, None, :] + 1
    grid[:, 3] = TPAD - tile[:, None, :]
    grid[:, 2:] *= tile[:, None, None, :] < T
    return {
        "c_iota": np.broadcast_to(np.arange(P, dtype=np.float32), (P, P)).copy(),
        "c_ident": np.eye(P, dtype=np.float32),
        "c_wlo": np.broadcast_to(window, (P, W)).copy(),
        "c_nnode": -(window[None, :] + np.arange(P, dtype=np.float32)[:, None]),
        "c_pick": np.tile(np.eye(W, dtype=np.float32), (3, 1)),
        "c_tcon": grid,
    }


def kernel(x, src, dst, L0_gnn_Wq, L0_gnn_bq, L0_gnn_Wk, L0_gnn_bk, L0_gnn_Wv, L0_gnn_bv, L0_gnn_Wp, L0_gnn_bp,
           L0_gnn_ln_g, L0_gnn_ln_b, L0_gnn_W1, L0_gnn_b1, L0_gnn_W2, L0_gnn_b2,
           L1_gnn_W_s, L1_gnn_W_t, L1_gnn_W_attn, L1_gnn_W_fc, L1_gnn_b_fc):
    import concourse.bacc as bacc
    from concourse.bass_utils import run_bass_kernel_spmd

    a = {k: np.asarray(v) for k, v in locals().items() if k not in ("bacc", "run_bass_kernel_spmd")}
    x = np.zeros((NP, C), a["x"].dtype)
    x[:N_NODES] = a["x"]

    def edges(e):
        out = np.full((TPAD * P,), FAKE, e.dtype)
        out[:N_EDGES] = e
        return out.reshape(TPAD, P)

    def columns(v):
        return v.reshape(-1, P).T

    arrays = {
        "src": edges(a["src"]).T, "dst": edges(a["dst"]).T, "dst_r": edges(a["dst"]),
        "x": x, "xt": x.reshape(W, P, KC, P).transpose(0, 3, 2, 1),
        "wqkv": np.concatenate([a["L0_gnn_Wk"].T, a["L0_gnn_Wv"].T, a["L0_gnn_Wq"].T], axis=1),
        "bqkv": np.concatenate([a["L0_gnn_bk"], a["L0_gnn_bv"], a["L0_gnn_bq"]]),
        "wp": a["L0_gnn_Wp"].T, "bp": a["L0_gnn_bp"],
        "lng": columns(a["L0_gnn_ln_g"]), "lnb": columns(a["L0_gnn_ln_b"]),
        "w1": a["L0_gnn_W1"].T, "b1": columns(a["L0_gnn_b1"]), "w2": a["L0_gnn_W2"].T, "b2": a["L0_gnn_b2"],
        "wst": np.concatenate([a["L1_gnn_W_s"].T, a["L1_gnn_W_t"].T], axis=1),
        "attn": a["L1_gnn_W_attn"].reshape(C), "wfc": a["L1_gnn_W_fc"].T, "bfc": a["L1_gnn_b_fc"],
    }
    arrays.update(shape_constants())
    arrays = {f"in_{k}": np.ascontiguousarray(arrays[k]) for k in INPUTS}

    nc = bacc.Bacc("TRN2", target_bir_lowering=False, num_devices=1)
    io = {k: nc.dram_tensor(f"in_{k}", arrays[f"in_{k}"].shape, mybir.dt.from_np(arrays[f"in_{k}"].dtype), kind="ExternalInput").ap()
          for k in INPUTS}
    io["out"] = nc.dram_tensor("out", (N_NODES, C), F32, kind="ExternalOutput").ap()
    build(nc, io)
    return run_bass_kernel_spmd(nc, [arrays], core_ids=[0]).results[0]["out"]
```
